# Optimizing a Trainium2 kernel written in Bass

```python
import numpy as np
import jax
import jax.numpy as jnp

def _softmax(x, axis=-1):
    return jax.nn.softmax(x, axis=axis)

def _gelu(x):
    return jax.nn.gelu(x, approximate=True)

def _silu(x):
    return jax.nn.silu(x)

def _sigmoid(x):
    return jax.nn.sigmoid(x)

def _layernorm(x, axis=-1, eps=1e-05):
    m = jnp.mean(x, axis=axis, keepdims=True)
    v = jnp.var(x, axis=axis, keepdims=True)
    return (x - m) / jnp.sqrt(v + eps)

def _scatter_add(tgt, idx, src, axis=0):
    return tgt.at[idx].add(src)

def _segment_sum(src, seg, n):
    return jax.ops.segment_sum(src, seg, n)
kernel_name = 'mk_gnn_preln_d2_gnn_r32_6dccae'

def setup_inputs(seed: int=0):
    np.random.seed(seed)
    _w = jnp.asarray

    def _rec_inputs():
        import jax
        import jax.numpy as jnp
        _gk = jax.random.key(seed)
        x = -0.0003713 + 1 * jax.random.normal(jax.random.fold_in(_gk, 1), (3125, 128), jnp.float32)
        src = jax.random.randint(jax.random.fold_in(_gk, 2), (50000,), 0, 3125, jnp.int32)
        dst = jnp.minimum((3125 * jax.random.uniform(jax.random.fold_in(_gk, 3), (50000,)) ** 2.0).astype(jnp.int32), 99999)
        _o = jnp.argsort(dst, stable=True)
        src = src[_o]
        dst = dst[_o]
        edge_type_64 = jax.random.randint(jax.random.fold_in(_gk, 13), (50000,), 0, 64, jnp.int32)
        edge_weight1 = jax.random.uniform(jax.random.fold_in(_gk, 14), (50000, 1), jnp.float32, 0.0, 0.999998)
        return (x, src, dst, edge_type_64, edge_weight1)
    x, src, dst, edge_type_64, edge_weight1 = _rec_inputs()

    def _L0_gnn_setup():
        import jax, jax.numpy as jnp
        import numpy as np
        NUM_LAYERS = 3
        key = jax.random.key(seed)
        k1, k2, k3, k4, k5, k6 = jax.random.split(key, 6)
        N, E, IN, H, OUT = (3125, 50000, 128, 64, 128)
        x = jax.random.normal(k1, (N, IN), dtype=jnp.float32)
        edge_index = jax.random.randint(k2, (2, E), 0, N, dtype=jnp.int64)
        W_in = jax.random.normal(k3, (IN, H), dtype=jnp.float32) / np.sqrt(IN)
        b_in = jax.random.normal(k4, (H,), dtype=jnp.float32) * 0.01
        W_out = jax.random.normal(k5, (H, OUT), dtype=jnp.float32) / np.sqrt(H)
        b_out = jax.random.normal(k6, (OUT,), dtype=jnp.float32) * 0.01
        return {'x': x, 'edge_index': edge_index, 'W_in': W_in, 'b_in': b_in, 'W_out': W_out, 'b_out': b_out}
    _L0_gnn_all = _L0_gnn_setup()
    _L0_gnn_in = {k: v for k, v in _L0_gnn_all.items() if k in ('W_in', 'b_in', 'W_out', 'b_out')}
    del _L0_gnn_all

    def _L1_gnn_setup():
        import jax, jax.numpy as jnp
        import numpy as np
        N, E, IN, OUT, R, B = (625, 20000, 128, 128, 64, 16)
        key = jax.random.key(seed)
        ks = jax.random.split(key, 9)
        xav_w = float(np.sqrt(2.0 / (IN + OUT)))
        xav_c = float(np.sqrt(2.0 / (R + B)))
        return {'x': jax.random.normal(ks[0], (N, IN), jnp.float32), 'weight': jax.random.normal(ks[1], (B, IN, OUT), jnp.float32) * xav_w, 'w_comp': jax.random.normal(ks[2], (R, B), jnp.float32) * xav_c, 'h_bias': jnp.zeros((OUT,), jnp.float32), 'loop_weight': jax.random.normal(ks[3], (IN, OUT), jnp.float32) * xav_w, 'norm': jax.random.uniform(ks[4], (E, 1), jnp.float32), 'src': jax.random.randint(ks[5], (E,), 0, N, jnp.int32), 'dst': jax.random.randint(ks[6], (E,), 0, N, jnp.int32), 'etypes': jax.random.randint(ks[7], (E,), 0, R, jnp.int32)}
    _L1_gnn_all = _L1_gnn_setup()
    _L1_gnn_in = {k: v for k, v in _L1_gnn_all.items() if k in ('weight', 'w_comp', 'h_bias', 'loop_weight')}
    del _L1_gnn_all
    return {'x': x, 'src': src, 'dst': dst, 'edge_type_64': edge_type_64, 'edge_weight1': edge_weight1, 'L0_gnn_W_in': _L0_gnn_in['W_in'], 'L0_gnn_b_in': _L0_gnn_in['b_in'], 'L0_gnn_W_out': _L0_gnn_in['W_out'], 'L0_gnn_b_out': _L0_gnn_in['b_out'], 'L1_gnn_weight': _L1_gnn_in['weight'], 'L1_gnn_w_comp': _L1_gnn_in['w_comp'], 'L1_gnn_h_bias': _L1_gnn_in['h_bias'], 'L1_gnn_loop_weight': _L1_gnn_in['loop_weight']}

def reference(x, src, dst, edge_type_64, edge_weight1, L0_gnn_W_in, L0_gnn_b_in, L0_gnn_W_out, L0_gnn_b_out, L1_gnn_weight, L1_gnn_w_comp, L1_gnn_h_bias, L1_gnn_loop_weight):
    import jax
    import jax.numpy as jnp

    def _L0_gnn_ref(x, edge_index, W_in, b_in, W_out, b_out):
        import jax, jax.numpy as jnp
        import numpy as np
        NUM_LAYERS = 3
        N = x.shape[0]
        row, col = (edge_index[0], edge_index[1])
        h = x @ W_in + b_in
        deg = jax.ops.segment_sum(jnp.ones(row.shape[0], dtype=h.dtype), row, num_segments=N)
        deg_inv_sqrt = jnp.where(deg > 0, jax.lax.rsqrt(jnp.maximum(deg, 1.0)) * jnp.where(deg > 0, 1.0, 0.0), 0.0)
        edge_weight = deg_inv_sqrt[row] * deg_inv_sqrt[col]
        acc = h
        cur = h
        for _ in range(NUM_LAYERS):
            msgs = cur[col] * edge_weight[:, None]
            cur = jax.ops.segment_sum(msgs, row, num_segments=N)
            acc = acc + cur
        final = acc / (NUM_LAYERS + 1)
        return final @ W_out + b_out

    def _L1_gnn_ref(x, weight, w_comp, h_bias, loop_weight, norm, src, dst, etypes):
        import jax, jax.numpy as jnp
        import numpy as np
        N, E, IN, OUT, R, B = (625, 20000, 128, 128, 64, 16)
        W_rel = jnp.einsum('rb,bio->rio', w_comp, weight)
        h_all = jnp.einsum('ni,rio->nro', x, W_rel)
        msg = h_all[src, etypes] * norm
        agg = jax.ops.segment_sum(msg, dst, num_segments=x.shape[0])
        out = agg + h_bias + x @ loop_weight
        return jax.nn.relu(out)
    edge_index = jnp.stack([src, dst])
    h = jnp.maximum(_layernorm(x, axis=-1), 0.0)
    x = x + _L0_gnn_ref(h, edge_index, L0_gnn_W_in, L0_gnn_b_in, L0_gnn_W_out, L0_gnn_b_out)
    h = jnp.maximum(_layernorm(x, axis=-1), 0.0)
    x = x + _L1_gnn_ref(h, L1_gnn_weight, L1_gnn_w_comp, L1_gnn_h_bias, L1_gnn_loop_weight, edge_weight1, src, dst, edge_type_64)
    return x

_drawn_inputs = setup_inputs


def setup_inputs(seed=0):
    import zlib

    import numpy as np

    out = dict(_drawn_inputs(seed))
    spreads = {'L1_gnn_h_bias': (0.0, 0.1)}
    factors = {'L0_gnn_b_in': 4.105, 'L0_gnn_b_out': 4.963}
    for name, (base, spread) in spreads.items():
        noise = np.random.default_rng([zlib.crc32(name.encode()), seed]).standard_normal(out[name].shape)
        drawn = base * np.exp(spread * noise) if base else spread * noise
        out[name] = jnp.asarray(drawn.astype(out[name].dtype))
    for name, factor in factors.items():
        out[name] = (out[name] * factor).astype(out[name].dtype)
    return out
```

```python
from contextlib import ExitStack

import numpy as np

import concourse.bass as bass
from concourse import mybir

F32 = mybir.dt.float32
BF16 = mybir.dt.bfloat16
I32 = mybir.dt.int32
I16 = mybir.dt.int16
U16 = mybir.dt.uint16
ALU = mybir.AluOpType
ACT = mybir.ActivationFunctionType
AX = mybir.AxisListType
ds = bass.ds

P = 128
N = 3125
E = 50000
FEAT = 128
HID = 64
BASES = 16
TYPES = 64
LAYERS = 3
EPS = 1e-5

NG = -(-N // P)
NPAD = NG * P
NT = -(-E // P)
TAIL = E - (NT - 1) * P
TC = -(-NT // P)
WIN = 16
WPG = P // WIN
NW = NG * WPG
HI = P // WIN
LO = NPAD // HI
S = NT + NW - 1
U = 10
TURNS = S // U
HALF = S // 2
RING = 4
FAR = 60000
CCH = 4
GCH = 16
GRING = 2 * GCH
BATCH = 5
NB = NG // BATCH
PC0 = 11
CT_TURNS = -(-NT // (2 * CCH))
H_TURNS = -(-NG // 4)
PART = 3 * HID
SLOT = 256


def tiles_view(flat, c0, c1):
    return flat[c0 * P * P:c1 * P * P].rearrange("(c t e) -> t c e", t=P, e=P)


def build(nc, x, src, dst, etype, norm, W_in, b_in, W_out, b_out, weight, w_comp, h_bias, loop_w, out):
    assert TURNS * U == S
    ctx = ExitStack()
    with ctx:
        def sb(name, shape, dt):
            return ctx.enter_context(nc.sbuf_tensor(name, shape, dt))

        def sem(name):
            return ctx.enter_context(nc.semaphore(name))

        coef_dram = nc.dram_tensor("coef_dram", (P, (NT + 1) * BASES), F32, kind="Internal").ap()
        h2_dram = nc.dram_tensor("h2_dram", (NPAD, FEAT), F32, kind="Internal").ap()

        CT = sb("CT", [P, NG, NPAD], BF16)
        u0 = sb("u0", [P, NG, PART], BF16)
        ohbuf = sb("ohbuf", [P, U * (P + LO)], BF16)
        acc = sb("acc", [P, NG, HID], F32)
        stage = sb("stage", [P, RING, LO], BF16)
        keyP = sb("keyP", [P, S], F32)
        loP = sb("loP", [P, S], F32)
        dlP = sb("dlP", [P, S], F32)
        src_col = sb("src_col", [P, NT], I32)
        iota16 = sb("iota16", [P, LO], I16)
        ident = sb("ident", [P, P], F32)
        ones_bf = sb("ones_bf", [P, P], BF16)
        zeros = sb("zeros", [P, LO], F32)
        dis = sb("dis", [P, NG], F32)
        small = sb("small", [P, 8, NG], F32)
        win_sb = sb("win_sb", [P, HID], F32)
        bin_sb = sb("bin_sb", [P, HID], F32)
        typ = sb("typ", [TYPES, 1], F32)
        wc_sb = sb("wc_sb", [TYPES, BASES], F32)
        coef_out = sb("coef_out", [P, 2 * CCH * BASES], F32)
        zero_bf = sb("zero_bf", [P, 512], BF16)
        idx_st = sb("idx_st", [P, 2, GCH], I32)
        tab_pe = sb("tab_pe", [1, TURNS, 2, U], U16)
        tab_dve = sb("tab_dve", [1, TURNS, 3, U], U16)
        tab_end = sb("tab_end", [1, NW], U16)
        tab_grp = sb("tab_grp", [1, TURNS + 1], U16)
        tab_tile = sb("tab_tile", [1, TC * P], U16)

        ohA = ohbuf[:, 0:U * P].rearrange("p (u k) -> p u k", u=U)
        ohB = ohbuf[:, U * P:].rearrange("p (u k) -> p u k", u=U)
        u1 = ohbuf[:, 0:NG * PART].rearrange("p (g k) -> p g k", g=NG)
        cbuf = u0[:, :, :].rearrange("p g k -> p (g k)")[0:TYPES, 0:4 * 2 * CCH * P].bitcast(F32)
        cbuf = cbuf.rearrange("p (b two e) -> p b two e", b=2, two=2)

        ps = ctx.enter_context(nc.psum_tensor("ps", [P, 8, 512], F32))
        psf = ps[:, :, :].rearrange("p b n -> p (b n)")

        late = CT[:, :, :].rearrange("p g n -> p (g n)").bitcast(F32)
        at = [0]

        def carve(n):
            at[0] += n
            assert at[0] <= late.shape[1]
            return late[:, at[0] - n:at[0]]

        dst_i = carve(TC * P).bitcast(I32).rearrange("p (c e) -> p c e", c=TC)
        src_i = carve(TC * P).bitcast(I32).rearrange("p (c e) -> p c e", c=TC)
        dst_f = carve(TC * P).rearrange("p (c e) -> p c e", c=TC)
        src_f = carve(TC * P).rearrange("p (c e) -> p c e", c=TC)
        hi_f = carve(TC * P).rearrange("p (c e) -> p c e", c=TC)
        key_f = carve(TC * P).rearrange("p (c e) -> p c e", c=TC)
        lo_f = carve(TC * P).rearrange("p (c e) -> p c e", c=TC)
        iota_i = carve(S).bitcast(I32)
        iota_f = carve(S)
        stepM = carve(TC * S // 2).bitcast(BF16).rearrange("p (c s) -> p c s", c=TC)
        onT = carve(TC * S).rearrange("p (c s) -> p c s", c=TC)
        ts_f = carve(S)
        ws_f = carve(S)
        row_i = carve(S).bitcast(I32)
        row_m = carve(S).bitcast(I32)
        tidx_i = carve(TC).bitcast(I32)
        tidx = carve(TC)
        wf_i = carve(TC).bitcast(I32)
        wf = carve(TC)
        af = carve(TC)
        endM = carve(TC * NW // 2).bitcast(BF16).rearrange("p (c w) -> p c w", c=TC)
        end_f = carve(NW)
        grpM = carve(NG * (TURNS + 1)).rearrange("p (g n) -> p g n", g=NG)
        grp_f = carve(TURNS + 1)
        turn_f = carve(TURNS + 1)
        x_sb = carve(NG * FEAT).rearrange("p (g f) -> p g f", g=NG)
        hT = carve(2 * 4 * P).rearrange("p (b n) -> p b n", b=2)
        stats = carve(NG * 6).rearrange("p (g k) -> p g k", g=NG)
        mv = carve(NG * 2).rearrange("p (g k) -> p g k", g=NG)

        after = CT[:, :, :].rearrange("p g n -> p (g n)").bitcast(F32)
        at2 = [0]

        def carve2(n):
            at2[0] += n
            assert at2[0] <= after.shape[1]
            return after[:, at2[0] - n:at2[0]]

        coef = carve2(NT * BASES).rearrange("p (t b) -> p t b", b=BASES)
        wrel = carve2(BASES * FEAT).rearrange("p (b o) -> p b o", b=BASES)
        loopw = carve2(FEAT)
        hb = carve2(1)
        wout = carve2(FEAT)[0:HID]
        bout = carve2(FEAT)
        x2 = carve2(NG * FEAT).rearrange("p (g f) -> p g f", g=NG)
        xb = carve2(NG * FEAT).rearrange("p (g f) -> p g f", g=NG)
        h2 = carve2(NG * FEAT).rearrange("p (g f) -> p g f", g=NG)
        relu_out = carve2(NPAD)
        fT = carve2(BATCH * P)[0:HID]
        h2T = carve2(NPAD)
        stats2 = carve2(NG * 6).rearrange("p (g k) -> p g k", g=NG)
        mv2 = carve2(NG * 2).rearrange("p (g k) -> p g k", g=NG)
        gring = carve2(GRING * FEAT).rearrange("p (r f) -> p r f", r=GRING)
        gpair = carve2(U * FEAT).rearrange("p (u f) -> p u f", u=U)
        kpair = carve2(U * WIN * BASES).rearrange("p (u d b) -> p u d b", u=U, b=BASES)
        zsb = carve2(2 * P * BASES).rearrange("p (h d b) -> p h d b", h=2, b=BASES)

        v_tmp = stage[:, :, :].rearrange("p r n -> p (r n)")[:, 0:4 * BATCH * HID].bitcast(F32)
        v_tmp = v_tmp.rearrange("p (k g h) -> p k g h", k=2, g=BATCH)

        ld_edge = sem("ld_edge")
        ld_par = sem("ld_par")
        ld_x = sem("ld_x")
        pool_c = sem("pool_c")
        dve_c = sem("dve_c")
        act_c = sem("act_c")
        pe_setup = sem("pe_setup")
        slots_free = sem("slots_free")
        oh_ready = sem("oh_ready")
        pairs_done = sem("pairs_done")
        staged = sem("staged")
        ct_in = [sem(f"ct_in{r}") for r in range(RING)]
        et_in = [sem(f"et_in{b}") for b in range(2)]
        typed = sem("typed")
        coef_mm = sem("coef_mm")
        coef_cp = sem("coef_cp")
        coef_st = sem("coef_st")
        tables_in = sem("tables_in")
        hmul = sem("hmul"); hread = sem("hread"); htrans = sem("htrans"); hcopied = sem("hcopied")
        setup_over = sem("setup_over"); deg_mm = sem("deg_mm"); act_n = sem("act_n"); idx_ok = sem("idx_ok")
        tail = sem("tail"); passed = sem("passed")
        deg_done = sem("deg_done")
        u_ready = sem("u_ready")
        prop_done = sem("prop_done")
        prop_read = sem("prop_read")
        fin_pe = sem("fin_pe")
        fin_dve = sem("fin_dve")
        fin_act = sem("fin_act")
        fin_pool = sem("fin_pool")
        h2_st = sem("h2_st")
        ld_two = sem("ld_two")
        ld_coef = sem("ld_coef")
        g_in = [sem(f"g_in{i}") for i in range(GRING)]
        gathered = sem("gathered")
        slots2 = sem("slots2")
        pair_in = sem("pair_in")
        pairs2 = sem("pairs2")
        zcopied = sem("zcopied")
        zgrp = sem("zgrp")
        routed = sem("routed")
        ogrp = sem("ogrp")
        ost = sem("ost")

        block = ctx.enter_context(nc.Block())

        @block.sync
        def _(sp):
            sp.wait_ge(pool_c, 4)
            full = TC - 1
            rest = NT - 1 - full * P
            for row, flat in ((dst_i, dst), (src_i, src)):
                sp.dma_start(row[:, 0:full, :], tiles_view(flat, 0, full)).then_inc(ld_edge, 16)
                sp.dma_start(row[0:rest, full, :],
                             flat[full * P * P:(NT - 1) * P].rearrange("(t e) -> t e", e=P)).then_inc(ld_edge, 16)
                sp.dma_start(row[rest:rest + 1, full, 0:TAIL],
                             flat[(NT - 1) * P:E].rearrange("(t e) -> t e", t=1)).then_inc(ld_edge, 16)
            sp.dma_start(x_sb[:, 0:NG - 1, :], x[0:(NG - 1) * P].rearrange("(g p) f -> p g f", p=P)).then_inc(ld_x, 16)
            sp.dma_start(x_sb[0:N - (NG - 1) * P, NG - 1, :], x[(NG - 1) * P:N]).then_inc(ld_x, 16)
            sp.dma_start(win_sb[:], W_in).then_inc(ld_par, 16)
            sp.dma_start(bin_sb[:], b_in.unsqueeze(0).broadcast_to([P, HID])).then_inc(ld_par, 16)
            sp.dma_start(wc_sb[:], w_comp).then_inc(ld_par, 16)

            with sp.Fori(0, NG) as g:
                for j in range(WPG):
                    sp.wait_ge(staged, g * WPG + (j + 1))
                    sp.dma_start(CT[WIN * j:WIN * (j + 1), ds(g, 1), :].rearrange("d a (h l) -> d (a h) l", h=HI),
                                 stage[:, j % RING, :]).then_inc(ct_in[j % RING], 16)

            sp.wait_ge(prop_done, LAYERS * NG)
            sp.dma_start(xb[:, 0:NG - 1, :], x[0:(NG - 1) * P].rearrange("(g p) f -> p g f", p=P)).then_inc(ld_two, 16)
            sp.wait_ge(fin_pool, 1)
            sp.dma_start(xb[0:N - (NG - 1) * P, NG - 1, :], x[(NG - 1) * P:N]).then_inc(ld_two, 16)
            sp.dma_start(wout[:], W_out).then_inc(ld_two, 16)
            sp.dma_start(bout[:], b_out.unsqueeze(0).broadcast_to([P, FEAT])).then_inc(ld_two, 16)
            sp.dma_start(loopw[:], loop_w).then_inc(ld_two, 16)
            sp.dma_start(hb[:], h_bias.unsqueeze(1)).then_inc(ld_two, 16)
            sp.dma_start(wrel[:], weight.rearrange("b i o -> i b o")).then_inc(ld_two, 16)
            sp.wait_ge(coef_st, 16 * CT_TURNS)
            sp.dma_start(coef[:], coef_dram[:, 0:NT * BASES]).then_inc(ld_coef, 16)
            for b in range(NB):
                sp.wait_ge(fin_act, 4 * b + 3)
                sp.dma_start(h2_dram[b * BATCH * P:(b + 1) * BATCH * P].rearrange("(g p) f -> p g f", p=P),
                             h2[:, b * BATCH:(b + 1) * BATCH, :]).then_inc(h2_st, 16)

            with sp.Fori(0, NT // GRING) as k:
                for i in range(GRING):
                    sp.wait_ge(g_in[i], (k + 1) * 16)
                    sp.sem_inc(gathered, 1)
            for i in range(NT % GRING):
                sp.wait_ge(g_in[i], 16 * (NT // GRING + 1))
                sp.sem_inc(gathered, 1)

            for b in range(NB):
                sp.wait_ge(ogrp, b + 1)
                lo, hi = b * BATCH, (b + 1) * BATCH
                if b < NB - 1:
                    sp.dma_start(out[lo * P:hi * P].rearrange("(g p) f -> p g f", p=P), h2[:, lo:hi, :]).then_inc(ost, 16)
                else:
                    sp.dma_start(out[lo * P:(hi - 1) * P].rearrange("(g p) f -> p g f", p=P),
                                 h2[:, lo:hi - 1, :]).then_inc(ost, 16)
                    sp.dma_start(out[(hi - 1) * P:N], h2[0:N - (hi - 1) * P, hi - 1, :]).then_inc(ost, 16)
            sp.wait_ge(ost, 16 * (NB + 1))

        @block.gpsimd
        def _(pool):
            pool.memset(dst_i[:, TC - 1, :], FAR).then_inc(pool_c, 1)
            pool.memset(src_i[:, TC - 1, :], 0).then_inc(pool_c, 1)
            pool.memset(x_sb[:, NG - 1, :], 0.0).then_inc(pool_c, 1)
            pool.memset(cbuf[:, :, :, :], 0.0).then_inc(pool_c, 1)
            pool.iota(iota_i[:], pattern=[[1, S]], base=0, channel_multiplier=0).then_inc(pool_c, 1)
            pool.iota(tidx_i[:], pattern=[[P, TC]], base=0, channel_multiplier=1).then_inc(pool_c, 1)
            pool.memset(ident[:], 0.0).then_inc(pool_c, 1)
            pool.wait_ge(pool_c, 7)
            pool.affine_select(out=ident[:], in_=ident[:], compare_op=ALU.not_equal, fill=1.0, base=0,
                               pattern=[[-1, P]], channel_multiplier=1).then_inc(pool_c, 1)
            pool.memset(ones_bf[:], 1.0).then_inc(pool_c, 1)
            pool.memset(zeros[:], 0.0).then_inc(pool_c, 1)
            pool.memset(zero_bf[:], 0.0).then_inc(pool_c, 1)
            pool.wait_ge(dve_c, 1)

            def load(turn, b, n=CCH * P):
                lo = turn * (2 * CCH * P) + b * CCH * P
                span = slice(lo, lo + n) if isinstance(turn, int) else ds(lo, n)
                pool.dma_start(cbuf[:, b, 0, 0:n].bitcast(I32),
                               etype[span].unsqueeze(0).broadcast_to([TYPES, n])).then_inc(et_in[b], 16)
                pool.dma_start(cbuf[:, b, 1, 0:n],
                               norm[span].unsqueeze(0).broadcast_to([TYPES, n])).then_inc(et_in[b], 16)

            def type_rows(turn):
                for b in range(2):
                    pool.wait_ge(et_in[b], turn * 32 + 32)
                    pool.sem_inc(passed, 1)
                    pool.tensor_scalar(cbuf[:, b, 0, :], cbuf[:, b, 0, :].bitcast(I32), typ[:, 0:1], None,
                                       ALU.is_equal).then_inc(pool_c, 1)
                for b in range(2):
                    pool.wait_ge(pool_c, turn * 2 + (PC0 + b + 1))
                    pool.tensor_tensor(cbuf[:, b, 1, :], cbuf[:, b, 0, :], cbuf[:, b, 1, :],
                                       ALU.mult).then_inc(typed, 1)

            def store(turn):
                pool.wait_ge(coef_cp, turn + 1)
                at = turn * (2 * CCH * BASES)
                span = slice(at, at + 2 * CCH * BASES) if isinstance(turn, int) else ds(at, 2 * CCH * BASES)
                pool.dma_start(coef_dram[:, span], coef_out[:]).then_inc(coef_st, 16)

            for b in range(2):
                load(0, b)
            with pool.Fori(0, CT_TURNS - 2) as c:
                type_rows(c)
                for b in range(2):
                    pool.wait_ge(coef_mm, c * 2 + (b + 1))
                    load(c + 1, b)
                store(c)
            type_rows(CT_TURNS - 2)
            for b in range(2):
                pool.wait_ge(coef_mm, 2 * (CT_TURNS - 2) + b + 1)
                load(CT_TURNS - 1, b, CCH * P if b == 0 else E - (2 * CT_TURNS - 1) * CCH * P)
            store(CT_TURNS - 2)
            type_rows(CT_TURNS - 1)
            store(CT_TURNS - 1)

            pool.wait_ge(prop_done, LAYERS * NG)
            pool.memset(xb[:, NG - 1, :], 0.0).then_inc(fin_pool, 1)
            pool.wait_ge(ld_two, 16 * 7)
            pool.tensor_tensor(xb[:, :, :], xb[:, :, :], bout.unsqueeze(1).broadcast_to([P, NG, FEAT]),
                               ALU.add).then_inc(fin_pool, 1)

            pool.wait_ge(h2_st, 16 * NB)

            def gather(k, half, n, wait):
                if wait:
                    pool.load(reg_t, tab_tile[0:1, ds(k * GCH - GCH, 1)])
                    pool.wait_ge(pair_in, pool.snap(reg_t))
                    pool.sem_inc(passed, 1)
                src_at = ds(k * GCH, n) if not isinstance(k, int) else slice(k * GCH, k * GCH + n)
                pool.tensor_copy(idx_st[:, half, 0:n], src_col[:, src_at]).then_inc(idx_ok, 1)
                pool.wait_ge(idx_ok, k + 1)
                pool.sem_inc(passed, 1)
                for i in range(n):
                    pool.indirect_dma_start(out=gring[:, half * GCH + i, :], out_offset=None, in_=h2_dram,
                                            in_offset=bass.IndirectOffsetOnAxis(ap=idx_st[:, half, i:i + 1], axis=0)
                                            ).then_inc(g_in[half * GCH + i], 16)

            reg_t = pool.alloc_register("tile_pos")
            gather(0, 0, GCH, False)
            gather(1, 1, GCH, False)
            with pool.Fori(1, NT // (2 * GCH)) as kk:
                for half in range(2):
                    gather(kk * 2 + half, half, GCH, True)
            gather(NT // GCH, 0, NT % GCH, True)

        @block.vector
        def _(dve):
            count = [0]

            def step(ins, wait=True):
                count[0] += 1
                ins.then_inc(dve_c, 1)
                if wait:
                    dve.wait_ge(dve_c, count[0])

            dve.wait_ge(pool_c, PC0)
            step(dve.tensor_copy(typ[:, 0:1], tidx_i[0:TYPES, 0:1]))
            step(dve.tensor_copy(iota_f[:], iota_i[:]), False)
            step(dve.tensor_copy(iota16[:], iota_i[:, 0:LO]), False)
            step(dve.tensor_copy(tidx[:], tidx_i[:]), False)
            dve.wait_ge(ld_edge, 16 * 6)
            step(dve.tensor_copy(dst_f[:], dst_i[:]), False)
            step(dve.tensor_copy(src_f[:], src_i[:]))
            step(dve.tensor_scalar(hi_f[:], src_f[:], float(LO), None, ALU.is_ge))
            for k in range(2, HI):
                step(dve.scalar_tensor_tensor(hi_f[:], src_f[:], float(k * LO), hi_f[:], ALU.is_ge, ALU.add))
            step(dve.scalar_tensor_tensor(key_f[:], dst_f[:], float(HI), hi_f[:], ALU.mult, ALU.add), False)
            step(dve.scalar_tensor_tensor(lo_f[:], hi_f[:], float(-LO), src_f[:], ALU.mult, ALU.add), False)
            step(dve.tensor_single_scalar(wf_i[:], dst_i[:, :, 0], WIN.bit_length() - 1, ALU.arith_shift_right))
            step(dve.tensor_copy(wf[:], wf_i[:]))
            step(dve.tensor_tensor(af[:], wf[:], tidx[:], ALU.add))
            step(dve.memset(af[0:1, 0:1], 0.0))
            step(dve.memset(wf[0:1, 0:1], float(FAR)))
            for c in range(TC):
                step(dve.tensor_scalar(stepM[:, c, :], iota_f[:], af[:, c:c + 1], None, ALU.is_ge), False)
                step(dve.tensor_scalar(endM[:, c, :], iota_f[:, 0:NW], wf[:, c:c + 1], None, ALU.is_ge), False)
            dve.wait_ge(dve_c, count[0])
            dve.sem_inc(tables_in, 1)
            dve.wait_ge(pe_setup, 1)
            for h in range(2):
                step(dve.tensor_scalar(ts_f[:, h * HALF:(h + 1) * HALF], ps[:, h, 0:HALF], -1.0, None, ALU.add), False)
            dve.wait_ge(dve_c, count[0])
            step(dve.tensor_tensor(ws_f[:], iota_f[:], ts_f[:], ALU.subtract), False)
            step(dve.tensor_tensor(end_f[:], ps[:, 2, 0:NW], iota_f[:, 0:NW], ALU.add), False)
            for c in range(TC):
                step(dve.tensor_scalar(onT[:, c, :], ts_f[:], tidx[:, c:c + 1], None, ALU.is_equal), False)
            dve.wait_ge(dve_c, count[0])
            dve.sem_inc(tables_in, 1)
            turn = lambda row: row[0:1, :].rearrange("p (c u) -> p c u", u=U)
            step(dve.tensor_scalar(tab_pe[:, :, 0, :], turn(ws_f), 1.0, None, ALU.add), False)
            step(dve.tensor_scalar(tab_dve[:, :, 0, :], turn(ts_f), 1.0, None, ALU.add), False)
            step(dve.tensor_copy(tab_dve[:, :, 1, :], turn(ts_f)), False)
            step(dve.tensor_scalar(tab_end[:], end_f[0:1, :], 1.0, None, ALU.add), False)
            step(dve.tensor_copy(row_i[0:1, :], ws_f[0:1, :]), False)
            step(dve.tensor_copy(row_m[0:1, :], ts_f[0:1, :]))
            step(dve.tensor_single_scalar(row_i[0:1, :], row_i[0:1, :], RING - 1, ALU.bitwise_and), False)
            step(dve.tensor_single_scalar(row_m[0:1, :], row_m[0:1, :], GRING - 1, ALU.bitwise_and))
            step(dve.tensor_copy(tab_pe[:, :, 1, :], turn(row_i)), False)
            step(dve.tensor_copy(tab_dve[:, :, 2, :], turn(row_m)), False)
            step(dve.tensor_scalar(turn_f[0:1, :], iota_f[0:1, 0:TURNS + 1], float(U), None, ALU.mult))
            ends = end_f[0:1, :].rearrange("p (g w) -> p g w", w=WPG)[:, :, WPG - 1]
            step(dve.tensor_tensor(grpM[0:1], turn_f[0:1, :].unsqueeze(1).broadcast_to([1, NG, TURNS + 1]),
                                   ends.unsqueeze(2).broadcast_to([1, NG, TURNS + 1]), ALU.is_gt))
            step(dve.tensor_reduce(grp_f[0:1, :], grpM[0:1].rearrange("p g c -> p c g"), AX.X, ALU.add))
            step(dve.tensor_copy(tab_grp[:], grp_f[0:1, :]), False)
            dve.wait_ge(pe_setup, 2)
            pairs_of = lambda b: ps[:, b:b + 2, 0:HALF]
            split = lambda row: row.rearrange("p (h s) -> p h s", h=2)
            step(dve.scalar_tensor_tensor(split(keyP[:]), split(ws_f), float(-WIN * HI), pairs_of(0), ALU.mult, ALU.add), False)
            step(dve.scalar_tensor_tensor(split(dlP[:]), split(ws_f), float(-WIN), pairs_of(2), ALU.mult, ALU.add), False)
            step(dve.tensor_copy(split(loP[:]), pairs_of(4)), False)
            step(dve.tensor_copy(src_col[:], ps[:, 6, 0:NT]), False)
            step(dve.tensor_scalar(tab_tile[:], ps[0:1, 7, :], 2.0, None, ALU.mult))
            dve.sem_inc(tables_in, 1)
            dve.wait_ge(ld_x, 32)
            norm_stats(dve, step, x_sb, stats, mv, 0, NG)
            dve.sem_inc(fin_dve, 1)
            dve.wait_ge(act_c, 1)
            norm_scales(dve, step, mv, small, 0, NG)
            dve.sem_inc(fin_dve, 1)
            dve.wait_ge(ld_par, 48)
            for q in range(-(-NG // 4)):
                n = min(4, NG - 4 * q)
                dve.wait_ge(hmul, q + 1)
                dve.tensor_tensor(acc[:, 4 * q:4 * q + n, :],
                                       ps[:, 2 + q % 2, 0:n * HID].rearrange("p (g h) -> p g h", h=HID),
                                       bin_sb[:, :].unsqueeze(1).broadcast_to([P, n, HID]), ALU.add).then_inc(hread, 1)
            dve.wait_ge(hread, H_TURNS)
            dve.sem_inc(setup_over, 1)

            def onehots(c, first=False, coefs=True):
                for u in range(U):
                    if not first and u % 5 == 0:
                        dve.wait_ge(pairs_done, c * U + (u + 5 - U))
                    s = c * U + u
                    col = slice(s, s + 1) if isinstance(s, int) else ds(s, 1)
                    dve.tensor_scalar(ohA[:, u, :], iota16[:, 0:P], keyP[:, col], None, ALU.is_equal).then_inc(oh_ready, 1)
                    dve.tensor_scalar(ohB[:, u, :], iota16[:], loP[:, col], None, ALU.is_equal).then_inc(oh_ready, 1)
                    if coefs and u == U - 1:
                        dve.wait_ge(coef_mm, c * 2 + 2)
                        if not first:
                            dve.wait_ge(coef_st, c * 16)
                        dve.tensor_copy(coef_out[:], ps[:, 4, 0:2 * CCH * BASES]).then_inc(coef_cp, 1)

            onehots(0, first=True)
            with dve.Fori(1, CT_TURNS) as c:
                onehots(c)
            with dve.Fori(CT_TURNS, TURNS) as c:
                onehots(c, coefs=False)

            dve.wait_ge(deg_done, 1)
            deg = ps[:, 7, 0:NG]
            step(dve.tensor_scalar(small[:, 2, :], deg, 1.0, None, ALU.max))
            dve.sem_inc(fin_dve, 1)
            step(dve.tensor_scalar(small[:, 3, :], deg, 0.0, None, ALU.is_gt), False)
            dve.wait_ge(act_c, 2 + NG)
            step(dve.reciprocal(small[:, 4, :], small[:, 4, :]))
            step(dve.tensor_tensor(dis[:], small[:, 4, :], small[:, 3, :], ALU.mult))

            def scaled(k, b):
                return v_tmp[:, k], dis[:, b * BATCH:(b + 1) * BATCH].unsqueeze(2).broadcast_to([P, BATCH, HID])

            def thirds(u, b):
                rows = u[:, b * BATCH:(b + 1) * BATCH, :].rearrange("p g (k h) -> p g k h", k=3)
                v, r = v_tmp[:, 0], v_tmp[:, 1]
                step(dve.tensor_copy(rows[:, :, 0, :], v))
                step(dve.tensor_tensor(r, v, rows[:, :, 0, :], ALU.subtract))
                step(dve.tensor_copy(rows[:, :, 1, :], r))
                step(dve.tensor_tensor(rows[:, :, 2, :], r, rows[:, :, 1, :], ALU.subtract))
                dve.sem_inc(u_ready, 1)

            for b in range(NB):
                v, dis_b = scaled(0, b)
                step(dve.tensor_tensor(v, acc[:, b * BATCH:(b + 1) * BATCH, :], dis_b, ALU.mult))
                thirds(u0, b)
            for layer in range(LAYERS):
                for b in range(NB):
                    got = layer * NB + b
                    dve.wait_ge(prop_done, (got + 1) * BATCH)
                    sums = psf[:, (got % 2) * 1536:(got % 2) * 1536 + BATCH * SLOT].rearrange(
                        "p (g k) -> p g k", k=SLOT)
                    v, dis_b = scaled(0, b)
                    r = v_tmp[:, 1]
                    step(dve.tensor_copy(r, sums[:, :, 2 * HID:3 * HID]))
                    step(dve.tensor_tensor(r, sums[:, :, HID:2 * HID], r, ALU.add))
                    step(dve.tensor_tensor(v, sums[:, :, 0:HID], r, ALU.add))
                    dve.sem_inc(prop_read, 1)
                    step(dve.tensor_tensor(v, v, dis_b, ALU.mult))
                    rows = acc[:, b * BATCH:(b + 1) * BATCH, :]
                    step(dve.tensor_tensor(rows, rows, v, ALU.add), False)
                    if layer < LAYERS - 1:
                        step(dve.tensor_tensor(v, v, dis_b, ALU.mult))
                        thirds(u1 if layer % 2 == 0 else u0, b)
            dve.wait_ge(dve_c, count[0])
            dve.sem_inc(fin_dve, 1)

            dve.wait_ge(fin_pool, 2)
            for b in range(NB):
                gs = slice(b * BATCH, (b + 1) * BATCH)
                dve.wait_ge(fin_pe, 3 * b + 2)
                step(dve.tensor_tensor(x2[:, gs, :], psf[:, 1024:1024 + BATCH * P].rearrange("p (g f) -> p g f", f=P),
                                       xb[:, gs, :], ALU.add))
                norm_stats(dve, step, x2, stats2, mv2, b * BATCH, (b + 1) * BATCH)
                dve.sem_inc(fin_dve, 1)
                dve.wait_ge(fin_act, 4 * b + 2)
                norm_scales(dve, step, mv2, small, b * BATCH, (b + 1) * BATCH)
                dve.sem_inc(fin_dve, 1)

            dve.wait_ge(ld_coef, 16)
            regs = [dve.alloc_register(f"pair{i}") for i in range(3 * U)]
            iota_w = iota16[:, 0:WIN].unsqueeze(2).broadcast_to([P, WIN, BASES])

            def operands(c, first=False):
                dve.load(regs, tab_dve[0:1, slice(c, c + 1) if isinstance(c, int) else ds(c, 1), :, :]
                         .rearrange("p c k u -> p (c k u)"))
                for u in range(U):
                    if not first and u % 5 == 0:
                        dve.wait_ge(pairs2, c * U + (u + 5 - U))
                    s = c * U + u
                    tile1 = dve.snap(regs[u], min_val=1, max_val=NT)
                    tile = dve.snap(regs[U + u], min_val=0, max_val=NT - 1)
                    slot = dve.snap(regs[2 * U + u], min_val=0, max_val=GRING - 1)
                    dve.wait_ge(gathered, tile1)
                    dve.tensor_copy(gpair[:, u:u + 1, :], gring[:, ds(slot, 1), :]).then_inc(pair_in, 1)
                    col = slice(s, s + 1) if isinstance(s, int) else ds(s, 1)
                    dve.scalar_tensor_tensor(kpair[:, u, :, :], iota_w, dlP[:, col],
                                             coef[:, ds(tile, 1), :].broadcast_to([P, WIN, BASES]),
                                             ALU.is_equal, ALU.mult).then_inc(pair_in, 1)

            operands(0, first=True)
            with dve.Fori(1, TURNS) as c:
                operands(c)

            for b in range(NB):
                gs = slice(b * BATCH, (b + 1) * BATCH)
                dve.wait_ge(tail, b + 1)
                at = (b % 2) * 1024
                dve.tensor_tensor(h2[:, gs, :], x2[:, gs, :],
                                  psf[:, at:at + BATCH * P].rearrange("p (g f) -> p g f", f=P), ALU.add).then_inc(ogrp, 1)

        @block.tensor
        def _(pe):
            pe.wait_ge(pool_c, PC0)
            pe.wait_ge(tables_in, 1)
            for h in range(2):
                for c in range(TC):
                    pe.matmul(ps[:, h, 0:HALF], ones_bf[:], stepM[:, c, h * HALF:(h + 1) * HALF],
                              start=(c == 0), stop=(c == TC - 1))
            for c in range(TC):
                last = pe.matmul(ps[:, 2, 0:NW], ones_bf[:], endM[:, c, :], start=(c == 0), stop=(c == TC - 1))
            last.then_inc(pe_setup, 1)
            pe.wait_ge(tables_in, 2)
            for k, field in enumerate((key_f, dst_f, lo_f)):
                for h in range(2):
                    for c in range(TC):
                        pe.matmul(ps[:, 2 * k + h, 0:HALF], field[:, c, :], onT[:, c, h * HALF:(h + 1) * HALF],
                                  start=(c == 0), stop=(c == TC - 1))
            for c in range(TC):
                n = min(P, NT - c * P)
                pe.matmul(ps[:, 6, c * P:c * P + n], src_f[:, c, :], ident[:, 0:n], start=True, stop=True)
            for c in range(TC):
                last = pe.matmul(ps[0:1, 7, c * P:(c + 1) * P], af[:, c:c + 1], ident[:], start=True, stop=True)
            last.then_inc(pe_setup, 1)

            pe.wait_ge(tables_in, 3)
            pe.wait_ge(ld_par, 48)
            for q in range(H_TURNS):
                n = min(4, NG - 4 * q)
                pe.wait_ge(act_c, 1 + 4 * q + n)
                if q >= 2:
                    pe.wait_ge(hcopied, q - 1)
                for i in range(n):
                    last = pe.transpose(ps[:, q % 2, i * P:(i + 1) * P], x_sb[:, 4 * q + i, :], ident[:])
                last.then_inc(htrans, 1)
                pe.wait_ge(hcopied, q + 1)
                if q >= 2:
                    pe.wait_ge(hread, q - 1)
                for i in range(n):
                    last = pe.matmul(ps[:, 2 + q % 2, i * HID:(i + 1) * HID], hT[:, q % 2, i * P:(i + 1) * P],
                                     win_sb[:], start=True, stop=True)
                last.then_inc(hmul, 1)

            pe.wait_ge(setup_over, 1)
            zb, zw = zero_bf[:, 0:P], zero_bf[:, :]
            for r in range(RING):
                pe.matmul(ps[:, r, :], zb, zw, start=True, stop=True).then_inc(slots_free, 1)

            regs = [pe.alloc_register(f"win{i}") for i in range(2 * U)]

            def slots(c):
                pe.load(regs, tab_pe[0:1, slice(c, c + 1) if isinstance(c, int) else ds(c, 1), :, :]
                        .rearrange("p c k u -> p (c k u)"))

            def count_pairs(c, coefs=True, first=False):
                slots(c)
                for u in range(U):
                    s = c * U + u
                    window1 = pe.snap(regs[u], min_val=1, max_val=NW + 1)
                    slot = pe.snap(regs[U + u], min_val=0, max_val=RING - 1)
                    pe.wait_ge(oh_ready, s * 2 + 2)
                    pe.wait_ge(slots_free, window1)
                    pe.matmul(ps[:, ds(slot, 1), 0:LO], ohA[:, u, :], ohB[:, u, :], start=False, stop=True,
                              skip_group_check=True).then_inc(pairs_done, 1)
                    if coefs and u == U // 2:
                        if not first:
                            pe.wait_ge(coef_cp, c)
                        for b in range(2):
                            pe.wait_ge(typed, c * 2 + (b + 1))
                            for i in range(CCH):
                                at = (b * CCH + i) * BASES
                                last = pe.matmul(ps[:, 4, at:at + BASES], cbuf[:, b, 1, i * P:(i + 1) * P],
                                                 wc_sb[:], start=True, stop=True)
                            last.then_inc(coef_mm, 1)

            count_pairs(0, first=True)
            with pe.Fori(1, CT_TURNS) as c:
                count_pairs(c)
            with pe.Fori(CT_TURNS, TURNS) as c:
                count_pairs(c, coefs=False)

            for r in range(RING):
                pe.wait_ge(ct_in[r], 16 * NW // RING)
            with pe.Fori(0, NG) as m:
                for k in range(NG):
                    last = pe.matmul(ps[:, 7, ds(m, 1)], CT[:, k, ds(m * P, P)], ones_bf[:, 0:1],
                                     start=(k == 0), stop=(k == NG - 1), skip_group_check=True)
                last.then_inc(deg_mm, 1)
            pe.wait_ge(deg_mm, NG)
            pe.sem_inc(deg_done, 1)

            for layer in range(LAYERS):
                u = u0 if layer % 2 == 0 else u1
                pe.wait_ge(u_ready, (layer + 1) * NB)
                for b in range(NB):
                    got = layer * NB + b
                    if got >= 2:
                        pe.wait_ge(prop_read, got - 1)
                    for i in range(BATCH):
                        m = b * BATCH + i
                        at = (got % 2) * 1536 + i * SLOT
                        for k in range(NG):
                            last = pe.matmul(psf[:, at:at + PART], CT[:, k, m * P:(m + 1) * P], u[:, k, :],
                                             start=(k == 0), stop=(k == NG - 1))
                        last.then_inc(prop_done, 1)

            pe.wait_ge(fin_dve, 4)
            pe.wait_ge(ld_two, 16 * 7)
            for b in range(NB):
                for i in range(BATCH):
                    last = pe.transpose(psf[0:HID, i * P:(i + 1) * P], acc[:, b * BATCH + i, :], ident[:])
                last.then_inc(fin_pe, 1)
                pe.wait_ge(fin_act, 4 * b + 1)
                if b:
                    pe.wait_ge(fin_dve, 3 + 2 * b)
                for i in range(BATCH):
                    last = pe.matmul(psf[:, 1024 + i * P:1024 + (i + 1) * P], fT[:, i * P:(i + 1) * P], wout[:],
                                     start=True, stop=True)
                last.then_inc(fin_pe, 1)
                pe.wait_ge(fin_act, 4 * b + 3)
                for i in range(BATCH):
                    last = pe.transpose(psf[:, 2048 + i * P:2048 + (i + 1) * P], h2[:, b * BATCH + i, :], ident[:])
                last.then_inc(fin_pe, 1)

            pe.wait_ge(fin_dve, 4 + 2 * NB)
            pe.wait_ge(fin_act, 4 * NB)
            for r in range(RING):
                pe.matmul(ps[:, r, :], zb, zw, start=True, stop=True).then_inc(slots2, 1)
            greg = [pe.alloc_register(f"grp{i}") for i in range(2)]

            def group_output(g):
                half = g % 2
                pe.wait_ge(zcopied, g * WPG + WPG)
                pe.wait_ge(routed, g + 1)
                bank = ps[:, ds(half + RING, 1), 0:P].rearrange("p a n -> p (a n)")
                for b in range(BASES):
                    rows = zsb[:, ds(half, 1), :, b].rearrange("p a d -> p (a d)")
                    pe.matmul(bank, wrel[:, b, :], rows, start=(b == 0), stop=False)
                pe.matmul(bank, loopw[:], h2T[:, ds(g * P, P)], start=False, stop=True).then_inc(zgrp, 1)

            def sum_pairs(c):
                slots(c)
                for u in range(U):
                    s = c * U + u
                    window1 = pe.snap(regs[u], min_val=1, max_val=NW + 1)
                    slot = pe.snap(regs[U + u], min_val=0, max_val=RING - 1)
                    pe.wait_ge(pair_in, s * 2 + 2)
                    pe.wait_ge(slots2, window1)
                    pe.matmul(ps[:, ds(slot, 1), 0:WIN * BASES], gpair[:, u, :],
                              kpair[:, u, :, :].rearrange("p d b -> p (d b)"), start=False, stop=True,
                              skip_group_check=True).then_inc(pairs2, 1)

            with pe.Fori(0, TURNS) as c:
                sum_pairs(c)
                pe.load(greg, tab_grp[0:1, ds(c, 2)])
                done = pe.snap(greg[0], min_val=0, max_val=NG)
                now = pe.snap(greg[1], min_val=0, max_val=NG)
                with pe.If(done < now):
                    with pe.Fori(done, now) as g:
                        group_output(g)
                with pe.Else():
                    pe.nop()
            for b in range(NB):
                pe.wait_ge(routed, 2 + NG)
                if b >= 2:
                    pe.wait_ge(ogrp, b - 1)
                for i in range(BATCH):
                    at = (b % 2) * 1024 + i * P
                    last = pe.transpose(psf[:, at:at + P], relu_out[:, (b * BATCH + i) * P:(b * BATCH + i + 1) * P], ident[:])
                last.then_inc(tail, 1)

        @block.scalar
        def _(act):
            act.wait_ge(fin_dve, 1)
            act.activation(small[:, 0, :], mv[:, :, 1], ACT.Sqrt).then_inc(act_c, 1)
            act.wait_ge(fin_dve, 2)
            for g in range(NG):
                act.activation(x_sb[:, g, :], x_sb[:, g, :], ACT.Relu, bias=small[:, 1, g:g + 1],
                               scale=small[:, 0, g:g + 1]).then_inc(act_c, 1)
            for q in range(H_TURNS):
                n = min(4, NG - 4 * q)
                act.wait_ge(htrans, q + 1)
                if q >= 2:
                    act.wait_ge(hmul, q - 1)
                act.copy(hT[:, q % 2, 0:n * P], ps[:, q % 2, 0:n * P]).then_inc(hcopied, 1)

            act.wait_ge(tables_in, 3)
            wreg = [act.alloc_register(f"end{i}") for i in range(WPG)]

            def copy_windows(g, first=False):
                act.load(wreg, tab_end[0:1, slice(0, WPG) if first else ds(g * WPG, WPG)])
                for j in range(WPG):
                    act.wait_ge(pairs_done, act.snap(wreg[j], min_val=1, max_val=S))
                    if not (first and j < RING):
                        act.wait_ge(ct_in[j % RING], g * 32 + (16 if j >= RING else 0))
                    act.copy(stage[:, j % RING, :], ps[:, j % RING, 0:LO]).then_inc(staged, 1)
                    act.wait_ge(staged, g * WPG + (j + 1))
                    act.copy(ps[:, j % RING, 0:LO], zeros[:]).then_inc(slots_free, 1)

            copy_windows(0, first=True)
            with act.Fori(1, NG) as g:
                copy_windows(g)

            act.wait_ge(fin_dve, 3)
            act.activation(small[:, 4, :], small[:, 2, :], ACT.Sqrt).then_inc(act_c, 1)

            for b in range(NB):
                act.wait_ge(fin_pe, 3 * b + 1)
                act.mul(fT[:], psf[0:HID, 0:BATCH * P], 1.0 / (LAYERS + 1)).then_inc(fin_act, 1)
                act.wait_ge(fin_dve, 5 + 2 * b)
                gs = slice(b * BATCH, (b + 1) * BATCH)
                act.activation(small[:, 0, gs], mv2[:, gs, 1], ACT.Sqrt).then_inc(fin_act, 1)
                act.wait_ge(fin_dve, 6 + 2 * b)
                for i in range(BATCH):
                    g = b * BATCH + i
                    last = act.activation(h2[:, g, :], x2[:, g, :], ACT.Relu, bias=small[:, 1, g:g + 1],
                                          scale=small[:, 0, g:g + 1])
                    last.then_inc(act_n, 1)
                act.wait_ge(act_n, (b + 1) * BATCH)
                act.sem_inc(fin_act, 1)
                act.wait_ge(fin_pe, 3 * b + 3)
                act.copy(h2T[:, b * BATCH * P:(b + 1) * BATCH * P], psf[:, 2048:2048 + BATCH * P]).then_inc(fin_act, 1)

            act.sem_inc(routed, 2)

            def copy_sums(g, half, wait=True):
                act.load(wreg, tab_end[0:1, ds(g * WPG, WPG) if wait else slice(g * WPG, (g + 1) * WPG)])
                for j in range(WPG):
                    act.wait_ge(pairs2, act.snap(wreg[j], min_val=1, max_val=S))
                    act.copy(zsb[:, half, j * WIN:(j + 1) * WIN, :].rearrange("p d b -> p (d b)"),
                             ps[:, j % RING, 0:WIN * BASES]).then_inc(zcopied, 1)
                    act.wait_ge(zcopied, g * WPG + (j + 1))
                    act.copy(ps[:, j % RING, 0:WIN * BASES], zeros[:, 0:WIN * BASES]).then_inc(slots2, 1)

            def route(g, half):
                act.wait_ge(zgrp, g + 1)
                at = slice(g * P, (g + 1) * P) if isinstance(g, int) else ds(g * P, P)
                act.activation(relu_out[:, at], ps[:, RING + half, 0:P], ACT.Relu, bias=hb[:, 0:1]).then_inc(routed, 1)

            copy_sums(0, 0, False)
            copy_sums(1, 1, False)
            with act.Fori(1, NG // 2) as q:
                for half in range(2):
                    route(q * 2 + (half - 2), half)
                    copy_sums(q * 2 + half, half)
            route(NG - 3, 0)
            copy_sums(NG - 1, 0, False)
            route(NG - 2, 1)
            route(NG - 1, 0)


def norm_stats(dve, step, rows, stats, mv, lo, hi):
    for g in range(lo, hi):
        step(dve.bn_stats(stats[:, g, :], rows[:, g, :]), g == hi - 1)
    for g in range(lo, hi):
        step(dve.bn_aggr(mv[:, g, :], stats[:, g, :]), g == hi - 1)
    step(dve.tensor_scalar(mv[:, lo:hi, 1], mv[:, lo:hi, 1], EPS, None, ALU.add))


def norm_scales(dve, step, mv, small, lo, hi):
    step(dve.reciprocal(small[:, 0, lo:hi], small[:, 0, lo:hi]))
    step(dve.scalar_tensor_tensor(small[:, 1, lo:hi], mv[:, lo:hi, 0], -1.0, small[:, 0, lo:hi], ALU.mult, ALU.mult))


_ORDER = ("x", "src", "dst", "edge_type_64", "edge_weight1", "L0_gnn_W_in", "L0_gnn_b_in", "L0_gnn_W_out",
          "L0_gnn_b_out", "L1_gnn_weight", "L1_gnn_w_comp", "L1_gnn_h_bias", "L1_gnn_loop_weight")


def kernel(**inputs):
    import concourse.bacc as bacc
    from concourse.bass_utils import run_bass_kernel_spmd

    nc = bacc.Bacc("TRN2", target_bir_lowering=False, num_devices=1)
    arrays, args = {}, []
    for name in _ORDER:
        a = np.ascontiguousarray(inputs[name])
        if name == "edge_weight1":
            a = a.reshape(-1)
        arrays[name] = a
        args.append(nc.dram_tensor(name, a.shape, mybir.dt.from_np(a.dtype), kind="ExternalInput").ap())
    out = nc.dram_tensor("out", (N, FEAT), F32, kind="ExternalOutput").ap()
    build(nc, *args, out)
    return run_bass_kernel_spmd(nc, [arrays], core_ids=[0]).results[0]["out"]
```

```python
from contextlib import ExitStack

import numpy as np

import concourse.bass as bass
from concourse import mybir

F32 = mybir.dt.float32
BF16 = mybir.dt.bfloat16
I32 = mybir.dt.int32
I16 = mybir.dt.int16
U16 = mybir.dt.uint16
ALU = mybir.AluOpType
ACT = mybir.ActivationFunctionType
AX = mybir.AxisListType
ds = bass.ds

P = 128
N = 3125
E = 50000
FEAT = 128
HID = 64
BASES = 16
TYPES = 64
LAYERS = 3
EPS = 1e-5

NG = -(-N // P)
NPAD = NG * P
NT = -(-E // P)
TAIL = E - (NT - 1) * P
TC = -(-NT // P)
WIN = 16
WPG = P // WIN
NW = NG * WPG
HI = P // WIN
LO = NPAD // HI
S = NT + NW - 1
U = 10
TURNS = S // U
HALF = S // 2
RING = 4
FAR = 60000
CCH = 8
CHALF = CCH * P // 2
CBUF = 4
GCH = 16
GRING = 2 * GCH
BATCH = 5
NB = NG // BATCH
PC0 = 11
CT_TURNS = -(-NT // CCH)
H_TURNS = -(-NG // 4)
PART = 3 * HID
AT = 320
SLOT = 256


def tiles_view(flat, c0, c1):
    return flat[c0 * P * P:c1 * P * P].rearrange("(c t e) -> t c e", t=P, e=P)


def build(nc, x, src, dst, etype, norm, W_in, b_in, W_out, b_out, weight, w_comp, h_bias, loop_w, out):
    assert TURNS * U == S
    ctx = ExitStack()
    with ctx:
        def sb(name, shape, dt):
            return ctx.enter_context(nc.sbuf_tensor(name, shape, dt))

        def sem(name):
            return ctx.enter_context(nc.semaphore(name))

        coef_dram = nc.dram_tensor("coef_dram", (P, CT_TURNS * CCH * BASES), F32, kind="Internal").ap()
        h2_dram = nc.dram_tensor("h2_dram", (NPAD, FEAT), F32, kind="Internal").ap()

        CT = sb("CT", [P, NG, NPAD], BF16)
        u0 = sb("u0", [P, NG, PART], BF16)
        ohbuf = sb("ohbuf", [P, U * (P + LO)], BF16)
        acc = sb("acc", [P, NG, HID], F32)
        stage = sb("stage", [P, RING, LO], BF16)
        keyP = sb("keyP", [P, S], F32)
        loP = sb("loP", [P, S], F32)
        dlP = sb("dlP", [P, S], F32)
        src_col = sb("src_col", [P, NT], I32)
        iota16 = sb("iota16", [P, LO], I16)
        ident = sb("ident", [P, P], F32)
        ones_bf = sb("ones_bf", [P, P], BF16)
        zeros = sb("zeros", [P, LO], F32)
        dis = sb("dis", [P, NG], F32)
        small = sb("small", [P, 8, NG], F32)
        typ = sb("typ", [P, 1], F32)
        norm_col = sb("norm_col", [P, NT + 1], F32)
        wc_sb = sb("wc_sb", [P, 2, BASES], F32)
        coef_out = sb("coef_out", [P, CCH * BASES], F32)
        idx_st = sb("idx_st", [P, 2, GCH], I32)
        tab_pe = sb("tab_pe", [1, TURNS, 2, U], U16)
        tab_dve = sb("tab_dve", [1, TURNS, 3, U], U16)
        tab_end = sb("tab_end", [1, NW], U16)
        tab_grp = sb("tab_grp", [1, TURNS + 1], U16)
        tab_tile = sb("tab_tile", [1, TC * P], U16)

        ohA = ohbuf[:, 0:U * P].rearrange("p (u k) -> p u k", u=U)
        ohB = ohbuf[:, U * P:].rearrange("p (u k) -> p u k", u=U)
        u1 = ohbuf[:, 0:NG * PART].rearrange("p (g k) -> p g k", g=NG)
        cbuf = u0[:, :, :].rearrange("p g k -> p (g k)")[:, 0:2 * CBUF * CHALF].bitcast(F32)
        cbuf = cbuf.rearrange("p (b e) -> p b e", b=CBUF)

        ps = ctx.enter_context(nc.psum_tensor("ps", [P, 8, 512], F32))
        psf = ps[:, :, :].rearrange("p b n -> p (b n)")

        late = CT[:, :, :].rearrange("p g n -> p (g n)").bitcast(F32)
        at = [0]

        def carve(n):
            at[0] += n
            assert at[0] <= late.shape[1]
            return late[:, at[0] - n:at[0]]

        dst_i = carve(TC * P).bitcast(I32).rearrange("p (c e) -> p c e", c=TC)
        src_i = carve(TC * P).bitcast(I32).rearrange("p (c e) -> p c e", c=TC)
        norm_f = carve(TC * P).rearrange("p (c e) -> p c e", c=TC)
        dst_f = carve(TC * P).rearrange("p (c e) -> p c e", c=TC)
        src_f = carve(TC * P).rearrange("p (c e) -> p c e", c=TC)
        hi_f = carve(TC * P).rearrange("p (c e) -> p c e", c=TC)
        key_f = carve(TC * P).rearrange("p (c e) -> p c e", c=TC)
        lo_f = carve(TC * P).rearrange("p (c e) -> p c e", c=TC)
        iota_i = carve(S).bitcast(I32)
        iota_f = carve(S)
        stepM = carve(TC * S // 2).bitcast(BF16).rearrange("p (c s) -> p c s", c=TC)
        onT = carve(TC * S).rearrange("p (c s) -> p c s", c=TC)
        ts_f = carve(S)
        ws_f = carve(S)
        row_i = carve(S).bitcast(I32)
        row_m = carve(S).bitcast(I32)
        tidx_i = carve(TC).bitcast(I32)
        tidx = carve(TC)
        wf_i = carve(TC).bitcast(I32)
        wf = carve(TC)
        af = carve(TC)
        endM = carve(TC * NW // 2).bitcast(BF16).rearrange("p (c w) -> p c w", c=TC)
        end_f = carve(NW)
        grpM = carve(NG * (TURNS + 1)).rearrange("p (g n) -> p g n", g=NG)
        grp_f = carve(TURNS + 1)
        turn_f = carve(TURNS + 1)
        x_sb = carve(NG * FEAT).rearrange("p (g f) -> p g f", g=NG)
        hT = carve(2 * 4 * P).rearrange("p (b n) -> p b n", b=2)
        stats = carve(NG * 6).rearrange("p (g k) -> p g k", g=NG)
        mv = carve(NG * 2).rearrange("p (g k) -> p g k", g=NG)

        typ_i = carve(1).bitcast(I32)
        win_sb = carve(HID)
        bin_sb = carve(HID)

        after = CT[:, :, :].rearrange("p g n -> p (g n)").bitcast(F32)
        at2 = [0]

        def carve2(n):
            at2[0] += n
            assert at2[0] <= after.shape[1]
            return after[:, at2[0] - n:at2[0]]

        coef = carve2(NT * BASES).rearrange("p (t b) -> p t b", b=BASES)
        wrel = carve2(BASES * FEAT).rearrange("p (b o) -> p b o", b=BASES)
        loopw = carve2(FEAT)
        hb = carve2(1)
        wout = carve2(FEAT)[0:HID]
        bout = carve2(FEAT)
        x2 = carve2(NG * FEAT).rearrange("p (g f) -> p g f", g=NG)
        xb = carve2(NG * FEAT).rearrange("p (g f) -> p g f", g=NG)
        h2 = carve2(NG * FEAT).rearrange("p (g f) -> p g f", g=NG)
        relu_out = carve2(NPAD)
        fT = carve2(BATCH * P)[0:HID]
        h2T = carve2(NPAD)
        stats2 = carve2(NG * 6).rearrange("p (g k) -> p g k", g=NG)
        mv2 = carve2(NG * 2).rearrange("p (g k) -> p g k", g=NG)
        gring = carve2(GRING * FEAT).rearrange("p (r f) -> p r f", r=GRING)
        gpair = carve2(U * FEAT).rearrange("p (u f) -> p u f", u=U)
        kpair = carve2(U * WIN * BASES).rearrange("p (u d b) -> p u d b", u=U, b=BASES)
        zsb = carve2(2 * P * BASES).rearrange("p (h d b) -> p h d b", h=2, b=BASES)

        v_tmp = stage[:, :, :].rearrange("p r n -> p (r n)")[:, 0:4 * BATCH * HID].bitcast(F32)
        v_tmp = v_tmp.rearrange("p (k g h) -> p k g h", k=2, g=BATCH)

        ld_edge = sem("ld_edge")
        ld_par = sem("ld_par")
        ld_x = sem("ld_x")
        pool_c = sem("pool_c")
        dve_c = sem("dve_c")
        act_c = sem("act_c")
        pe_setup = sem("pe_setup")
        slots_free = sem("slots_free")
        oh_ready = sem("oh_ready")
        pairs_done = sem("pairs_done")
        staged = sem("staged")
        ct_in = [sem(f"ct_in{r}") for r in range(RING)]
        et_in = [sem(f"et_in{b}") for b in range(CBUF)]
        typed = sem("typed")
        coef_mm = sem("coef_mm")
        coef_cp = sem("coef_cp")
        coef_st = sem("coef_st")
        tables_in = sem("tables_in")
        hmul = sem("hmul"); hread = sem("hread"); htrans = sem("htrans"); hcopied = sem("hcopied")
        setup_over = sem("setup_over"); deg_mm = sem("deg_mm"); act_n = sem("act_n"); idx_ok = sem("idx_ok")
        tail = sem("tail"); passed = sem("passed")
        deg_done = sem("deg_done")
        u_ready = sem("u_ready")
        prop_done = sem("prop_done")
        prop_read = sem("prop_read")
        fin_pe = sem("fin_pe")
        fin_dve = sem("fin_dve")
        fin_act = sem("fin_act")
        fin_pool = sem("fin_pool")
        h2_st = sem("h2_st")
        ld_two = sem("ld_two")
        ld_coef = sem("ld_coef")
        g_in = [sem(f"g_in{i}") for i in range(GRING)]
        gathered = sem("gathered")
        slots2 = sem("slots2")
        pair_in = sem("pair_in")
        pairs2 = sem("pairs2")
        zcopied = sem("zcopied")
        zgrp = sem("zgrp")
        routed = sem("routed")
        ogrp = sem("ogrp")
        ost = sem("ost")

        block = ctx.enter_context(nc.Block())

        @block.sync
        def _(sp):
            sp.wait_ge(pool_c, 5)
            full = TC - 1
            rest = NT - 1 - full * P
            for row, flat in ((dst_i, dst), (src_i, src), (norm_f, norm)):
                sp.dma_start(row[:, 0:full, :], tiles_view(flat, 0, full)).then_inc(ld_edge, 16)
                sp.dma_start(row[0:rest, full, :],
                             flat[full * P * P:(NT - 1) * P].rearrange("(t e) -> t e", e=P)).then_inc(ld_edge, 16)
                sp.dma_start(row[rest:rest + 1, full, 0:TAIL],
                             flat[(NT - 1) * P:E].rearrange("(t e) -> t e", t=1)).then_inc(ld_edge, 16)
            sp.dma_start(x_sb[:, 0:NG - 1, :], x[0:(NG - 1) * P].rearrange("(g p) f -> p g f", p=P)).then_inc(ld_x, 16)
            sp.dma_start(x_sb[0:N - (NG - 1) * P, NG - 1, :], x[(NG - 1) * P:N]).then_inc(ld_x, 16)
            sp.dma_start(win_sb[:], W_in).then_inc(ld_par, 16)
            sp.dma_start(bin_sb[:], b_in.unsqueeze(0).broadcast_to([P, HID])).then_inc(ld_par, 16)
            for h in range(2):
                sp.dma_start(wc_sb[h * TYPES:(h + 1) * TYPES, h, :], w_comp).then_inc(ld_par, 16)

            with sp.Fori(0, NG) as g:
                for j in range(WPG):
                    sp.wait_ge(staged, g * WPG + (j + 1))
                    sp.dma_start(CT[WIN * j:WIN * (j + 1), ds(g, 1), :].rearrange("d a (h l) -> d (a h) l", h=HI),
                                 stage[:, j % RING, :]).then_inc(ct_in[j % RING], 16)

            sp.wait_ge(prop_done, LAYERS * NG)
            sp.dma_start(xb[:, 0:NG - 1, :], x[0:(NG - 1) * P].rearrange("(g p) f -> p g f", p=P)).then_inc(ld_two, 16)
            sp.wait_ge(fin_pool, 1)
            sp.dma_start(xb[0:N - (NG - 1) * P, NG - 1, :], x[(NG - 1) * P:N]).then_inc(ld_two, 16)
            sp.dma_start(wout[:], W_out).then_inc(ld_two, 16)
            sp.dma_start(bout[:], b_out.unsqueeze(0).broadcast_to([P, FEAT])).then_inc(ld_two, 16)
            sp.dma_start(loopw[:], loop_w).then_inc(ld_two, 16)
            sp.dma_start(hb[:], h_bias.unsqueeze(1)).then_inc(ld_two, 16)
            sp.dma_start(wrel[:], weight.rearrange("b i o -> i b o")).then_inc(ld_two, 16)
            sp.wait_ge(coef_st, 16 * CT_TURNS)
            sp.dma_start(coef[:], coef_dram[:, 0:NT * BASES]).then_inc(ld_coef, 16)
            for b in range(NB):
                sp.wait_ge(fin_act, 4 * b + 3)
                sp.dma_start(h2_dram[b * BATCH * P:(b + 1) * BATCH * P].rearrange("(g p) f -> p g f", p=P),
                             h2[:, b * BATCH:(b + 1) * BATCH, :]).then_inc(h2_st, 16)

            with sp.Fori(0, NT // GRING) as k:
                for i in range(GRING):
                    sp.wait_ge(g_in[i], (k + 1) * 16)
                    sp.sem_inc(gathered, 1)
            for i in range(NT % GRING):
                sp.wait_ge(g_in[i], 16 * (NT // GRING + 1))
                sp.sem_inc(gathered, 1)

            for b in range(NB):
                sp.wait_ge(ogrp, b + 1)
                lo, hi = b * BATCH, (b + 1) * BATCH
                if b < NB - 1:
                    sp.dma_start(out[lo * P:hi * P].rearrange("(g p) f -> p g f", p=P), h2[:, lo:hi, :]).then_inc(ost, 16)
                else:
                    sp.dma_start(out[lo * P:(hi - 1) * P].rearrange("(g p) f -> p g f", p=P),
                                 h2[:, lo:hi - 1, :]).then_inc(ost, 16)
                    sp.dma_start(out[(hi - 1) * P:N], h2[0:N - (hi - 1) * P, hi - 1, :]).then_inc(ost, 16)
            sp.wait_ge(ost, 16 * (NB + 1))

        @block.gpsimd
        def _(pool):
            pool.memset(dst_i[:, TC - 1, :], FAR).then_inc(pool_c, 1)
            pool.memset(src_i[:, TC - 1, :], 0).then_inc(pool_c, 1)
            pool.memset(norm_f[:, TC - 1, :], 0.0).then_inc(pool_c, 1)
            pool.memset(x_sb[:, NG - 1, :], 0.0).then_inc(pool_c, 1)
            pool.memset(wc_sb[:], 0.0).then_inc(pool_c, 1)
            pool.iota(iota_i[:], pattern=[[1, S]], base=0, channel_multiplier=0).then_inc(pool_c, 1)
            pool.iota(tidx_i[:], pattern=[[P, TC]], base=0, channel_multiplier=1).then_inc(pool_c, 1)
            pool.memset(ident[:], 0.0).then_inc(pool_c, 1)
            pool.wait_ge(pool_c, 8)
            pool.affine_select(out=ident[:], in_=ident[:], compare_op=ALU.not_equal, fill=1.0, base=0,
                               pattern=[[-1, P]], channel_multiplier=1).then_inc(pool_c, 1)
            pool.memset(ones_bf[:], 1.0).then_inc(pool_c, 1)
            pool.memset(zeros[:], 0.0).then_inc(pool_c, 1)
            pool.wait_ge(dve_c, 2)

            def load_types(turn, b):
                lo = turn * (CCH * P)
                span = slice(lo, lo + CCH * P) if isinstance(turn, int) else ds(lo, CCH * P)
                pool.dma_start(cbuf[:, b, :].bitcast(I32),
                               etype[span].rearrange("(h e) -> h e", h=2).unsqueeze(1)
                               .broadcast_to([2, TYPES, CHALF])).then_inc(et_in[b], 16)

            def type_rows(b, loaded):
                pool.wait_ge(et_in[b], loaded)
                pool.sem_inc(passed, 1)
                pool.tensor_scalar(cbuf[:, b, :], cbuf[:, b, :].bitcast(I32), typ[:, 0:1], None,
                                   ALU.is_equal).then_inc(typed, 1)

            def store_coefs(turn):
                pool.wait_ge(coef_cp, turn + 1)
                at = turn * (CCH * BASES)
                span = slice(at, at + CCH * BASES) if isinstance(turn, int) else ds(at, CCH * BASES)
                pool.dma_start(coef_dram[:, span], coef_out[:]).then_inc(coef_st, 16)

            for b in range(CBUF):
                load_types(b, b)
            type_rows(0, 16)
            type_rows(1, 16)
            with pool.Fori(0, CT_TURNS // CBUF - 1) as q:
                for j in range(CBUF):
                    type_rows((j + 2) % CBUF, q * 16 + (16 * ((j + 2) // CBUF) + 16))
                    store_coefs(q * CBUF + j)
                    load_types(q * CBUF + (j + CBUF), j)
            last = CT_TURNS - 1
            assert last % CBUF == 0
            loads = 16 * (last // CBUF)
            type_rows(2, loads)
            store_coefs(last - 4)
            first_edge = last * CCH * P
            pool.dma_start(cbuf[0:TYPES, 0, :].bitcast(I32), etype[first_edge:first_edge + CHALF].unsqueeze(0)
                           .broadcast_to([TYPES, CHALF])).then_inc(et_in[0], 16)
            rest = E - first_edge - CHALF
            pool.dma_start(cbuf[TYPES:P, 0, 0:rest].bitcast(I32), etype[first_edge + CHALF:E].unsqueeze(0)
                           .broadcast_to([TYPES, rest])).then_inc(et_in[0], 16)
            type_rows(3, loads)
            store_coefs(last - 3)
            type_rows(0, loads + 32)
            for turn in range(last - 2, last + 1):
                store_coefs(turn)

            pool.wait_ge(prop_done, LAYERS * NG)
            pool.memset(xb[:, NG - 1, :], 0.0).then_inc(fin_pool, 1)
            pool.wait_ge(ld_two, 16 * 7)
            pool.tensor_tensor(xb[:, :, :], xb[:, :, :], bout.unsqueeze(1).broadcast_to([P, NG, FEAT]),
                               ALU.add).then_inc(fin_pool, 1)

            pool.wait_ge(h2_st, 16 * NB)

            def gather(k, half, n, wait):
                if wait:
                    pool.load(reg_t, tab_tile[0:1, ds(k * GCH - GCH, 1)])
                    pool.wait_ge(pair_in, pool.snap(reg_t))
                    pool.sem_inc(passed, 1)
                src_at = ds(k * GCH, n) if not isinstance(k, int) else slice(k * GCH, k * GCH + n)
                pool.tensor_copy(idx_st[:, half, 0:n], src_col[:, src_at]).then_inc(idx_ok, 1)
                pool.wait_ge(idx_ok, k + 1)
                pool.sem_inc(passed, 1)
                for i in range(n):
                    pool.indirect_dma_start(out=gring[:, half * GCH + i, :], out_offset=None, in_=h2_dram,
                                            in_offset=bass.IndirectOffsetOnAxis(ap=idx_st[:, half, i:i + 1], axis=0)
                                            ).then_inc(g_in[half * GCH + i], 16)

            reg_t = pool.alloc_register("tile_pos")
            gather(0, 0, GCH, False)
            gather(1, 1, GCH, False)
            with pool.Fori(1, NT // (2 * GCH)) as kk:
                for half in range(2):
                    gather(kk * 2 + half, half, GCH, True)
            gather(NT // GCH, 0, NT % GCH, True)

        @block.vector
        def _(dve):
            count = [0]

            def step(ins, wait=True):
                count[0] += 1
                ins.then_inc(dve_c, 1)
                if wait:
                    dve.wait_ge(dve_c, count[0])

            dve.wait_ge(pool_c, PC0)
            step(dve.tensor_single_scalar(typ_i[:], tidx_i[:, 0:1], TYPES - 1, ALU.bitwise_and))
            step(dve.tensor_copy(typ[:], typ_i[:]))
            step(dve.tensor_copy(iota_f[:], iota_i[:]), False)
            step(dve.tensor_copy(iota16[:], iota_i[:, 0:LO]), False)
            step(dve.tensor_copy(tidx[:], tidx_i[:]), False)
            dve.wait_ge(ld_edge, 16 * 9)
            step(dve.tensor_copy(dst_f[:], dst_i[:]), False)
            step(dve.tensor_copy(src_f[:], src_i[:]))
            step(dve.tensor_scalar(hi_f[:], src_f[:], float(LO), None, ALU.is_ge))
            for k in range(2, HI):
                step(dve.scalar_tensor_tensor(hi_f[:], src_f[:], float(k * LO), hi_f[:], ALU.is_ge, ALU.add))
            step(dve.scalar_tensor_tensor(key_f[:], dst_f[:], float(HI), hi_f[:], ALU.mult, ALU.add), False)
            step(dve.scalar_tensor_tensor(lo_f[:], hi_f[:], float(-LO), src_f[:], ALU.mult, ALU.add), False)
            step(dve.tensor_single_scalar(wf_i[:], dst_i[:, :, 0], WIN.bit_length() - 1, ALU.arith_shift_right))
            step(dve.tensor_copy(wf[:], wf_i[:]))
            step(dve.tensor_tensor(af[:], wf[:], tidx[:], ALU.add))
            step(dve.memset(af[0:1, 0:1], 0.0))
            step(dve.memset(wf[0:1, 0:1], float(FAR)))
            for c in range(TC):
                step(dve.tensor_scalar(stepM[:, c, :], iota_f[:], af[:, c:c + 1], None, ALU.is_ge), False)
                step(dve.tensor_scalar(endM[:, c, :], iota_f[:, 0:NW], wf[:, c:c + 1], None, ALU.is_ge), False)
            dve.wait_ge(dve_c, count[0])
            dve.sem_inc(tables_in, 1)
            dve.wait_ge(pe_setup, 1)
            for h in range(2):
                step(dve.tensor_scalar(ts_f[:, h * HALF:(h + 1) * HALF], ps[:, h, 0:HALF], -1.0, None, ALU.add), False)
            dve.wait_ge(dve_c, count[0])
            step(dve.tensor_tensor(ws_f[:], iota_f[:], ts_f[:], ALU.subtract), False)
            step(dve.tensor_tensor(end_f[:], ps[:, 2, 0:NW], iota_f[:, 0:NW], ALU.add), False)
            for c in range(TC):
                step(dve.tensor_scalar(onT[:, c, :], ts_f[:], tidx[:, c:c + 1], None, ALU.is_equal), False)
            dve.wait_ge(dve_c, count[0])
            dve.sem_inc(tables_in, 1)
            turn = lambda row: row[0:1, :].rearrange("p (c u) -> p c u", u=U)
            step(dve.tensor_scalar(tab_pe[:, :, 0, :], turn(ws_f), 1.0, None, ALU.add), False)
            step(dve.tensor_scalar(tab_dve[:, :, 0, :], turn(ts_f), 1.0, None, ALU.add), False)
            step(dve.tensor_copy(tab_dve[:, :, 1, :], turn(ts_f)), False)
            step(dve.tensor_scalar(tab_end[:], end_f[0:1, :], 1.0, None, ALU.add), False)
            step(dve.tensor_copy(row_i[0:1, :], ws_f[0:1, :]), False)
            step(dve.tensor_copy(row_m[0:1, :], ts_f[0:1, :]))
            step(dve.tensor_single_scalar(row_i[0:1, :], row_i[0:1, :], RING - 1, ALU.bitwise_and), False)
            step(dve.tensor_single_scalar(row_m[0:1, :], row_m[0:1, :], GRING - 1, ALU.bitwise_and))
            step(dve.tensor_copy(tab_pe[:, :, 1, :], turn(row_i)), False)
            step(dve.tensor_copy(tab_dve[:, :, 2, :], turn(row_m)), False)
            step(dve.tensor_scalar(turn_f[0:1, :], iota_f[0:1, 0:TURNS + 1], float(U), None, ALU.mult))
            ends = end_f[0:1, :].rearrange("p (g w) -> p g w", w=WPG)[:, :, WPG - 1]
            step(dve.tensor_tensor(grpM[0:1], turn_f[0:1, :].unsqueeze(1).broadcast_to([1, NG, TURNS + 1]),
                                   ends.unsqueeze(2).broadcast_to([1, NG, TURNS + 1]), ALU.is_gt))
            step(dve.tensor_reduce(grp_f[0:1, :], grpM[0:1].rearrange("p g c -> p c g"), AX.X, ALU.add))
            step(dve.tensor_copy(tab_grp[:], grp_f[0:1, :]), False)
            dve.wait_ge(pe_setup, 2)
            pairs_of = lambda b: ps[:, b:b + 2, 0:HALF]
            split = lambda row: row.rearrange("p (h s) -> p h s", h=2)
            step(dve.scalar_tensor_tensor(split(keyP[:]), split(ws_f), float(-WIN * HI), pairs_of(0), ALU.mult, ALU.add), False)
            step(dve.scalar_tensor_tensor(split(dlP[:]), split(ws_f), float(-WIN), pairs_of(2), ALU.mult, ALU.add), False)
            step(dve.tensor_copy(split(loP[:]), pairs_of(4)), False)
            step(dve.tensor_copy(src_col[:], ps[:, 6, 0:NT]), False)
            step(dve.tensor_copy(norm_col[:], ps[:, 7, 0:NT + 1]), False)
            step(dve.tensor_scalar(tab_tile[:].rearrange("p (c t) -> p c t", t=P), ps[0:1, 0:TC, AT:AT + P], 2.0,
                                   None, ALU.mult))
            dve.sem_inc(tables_in, 1)
            dve.wait_ge(ld_x, 32)
            norm_stats(dve, step, x_sb, stats, mv, 0, NG)
            dve.sem_inc(fin_dve, 1)
            dve.wait_ge(act_c, 1)
            norm_scales(dve, step, mv, small, 0, NG)
            dve.sem_inc(fin_dve, 1)
            dve.wait_ge(ld_par, 64)
            for q in range(-(-NG // 4)):
                n = min(4, NG - 4 * q)
                dve.wait_ge(hmul, q + 1)
                dve.tensor_tensor(acc[:, 4 * q:4 * q + n, :],
                                       ps[:, 2 + q % 2, 0:n * HID].rearrange("p (g h) -> p g h", h=HID),
                                       bin_sb[:, :].unsqueeze(1).broadcast_to([P, n, HID]), ALU.add).then_inc(hread, 1)
            dve.wait_ge(hread, H_TURNS)
            dve.sem_inc(setup_over, 1)

            def finish_coefs(c, first=False):
                dve.wait_ge(coef_mm, 1 if first else c + 1)
                if not first:
                    dve.wait_ge(coef_st, c * 16)
                tiles = slice(0, CCH) if first else ds(c * CCH, CCH)
                dve.tensor_tensor(coef_out[:].rearrange("p (t b) -> p t b", b=BASES),
                                  ps[:, 4, 0:CCH * BASES].rearrange("p (t b) -> p t b", b=BASES),
                                  norm_col[:, tiles].unsqueeze(2).broadcast_to([P, CCH, BASES]),
                                  ALU.mult).then_inc(coef_cp, 1)

            def onehots(c, coefs=True):
                first = isinstance(c, int) and c == 0
                for u in range(U):
                    if not first and u % 5 == 0:
                        dve.wait_ge(pairs_done, c * U + (u + 5 - U))
                    s = c * U + u
                    col = slice(s, s + 1) if isinstance(s, int) else ds(s, 1)
                    dve.tensor_scalar(ohA[:, u, :], iota16[:, 0:P], keyP[:, col], None, ALU.is_equal).then_inc(oh_ready, 1)
                    dve.tensor_scalar(ohB[:, u, :], iota16[:], loP[:, col], None, ALU.is_equal).then_inc(oh_ready, 1)
                    if coefs and u == U // 2:
                        finish_coefs(c - 1, isinstance(c, int))

            onehots(0, coefs=False)
            onehots(1)
            with dve.Fori(2, CT_TURNS + 1) as c:
                onehots(c)
            with dve.Fori(CT_TURNS + 1, TURNS) as c:
                onehots(c, coefs=False)

            dve.wait_ge(deg_done, 1)
            deg = ps[:, 7, 0:NG]
            step(dve.tensor_scalar(small[:, 2, :], deg, 1.0, None, ALU.max))
            dve.sem_inc(fin_dve, 1)
            step(dve.tensor_scalar(small[:, 3, :], deg, 0.0, None, ALU.is_gt), False)
            dve.wait_ge(act_c, 2 + NG)
            step(dve.reciprocal(small[:, 4, :], small[:, 4, :]))
            step(dve.tensor_tensor(dis[:], small[:, 4, :], small[:, 3, :], ALU.mult))

            def scaled(k, b):
                return v_tmp[:, k], dis[:, b * BATCH:(b + 1) * BATCH].unsqueeze(2).broadcast_to([P, BATCH, HID])

            def thirds(u, b):
                rows = u[:, b * BATCH:(b + 1) * BATCH, :].rearrange("p g (k h) -> p g k h", k=3)
                v, r = v_tmp[:, 0], v_tmp[:, 1]
                step(dve.tensor_copy(rows[:, :, 0, :], v))
                step(dve.tensor_tensor(r, v, rows[:, :, 0, :], ALU.subtract))
                step(dve.tensor_copy(rows[:, :, 1, :], r))
                step(dve.tensor_tensor(rows[:, :, 2, :], r, rows[:, :, 1, :], ALU.subtract))
                dve.sem_inc(u_ready, 1)

            for b in range(NB):
                v, dis_b = scaled(0, b)
                step(dve.tensor_tensor(v, acc[:, b * BATCH:(b + 1) * BATCH, :], dis_b, ALU.mult))
                thirds(u0, b)
            for layer in range(LAYERS):
                for b in range(NB):
                    got = layer * NB + b
                    dve.wait_ge(prop_done, (got + 1) * BATCH)
                    sums = psf[:, (got % 2) * 1536:(got % 2) * 1536 + BATCH * SLOT].rearrange(
                        "p (g k) -> p g k", k=SLOT)
                    v, dis_b = scaled(0, b)
                    r = v_tmp[:, 1]
                    step(dve.tensor_copy(r, sums[:, :, 2 * HID:3 * HID]))
                    step(dve.tensor_tensor(r, sums[:, :, HID:2 * HID], r, ALU.add))
                    step(dve.tensor_tensor(v, sums[:, :, 0:HID], r, ALU.add))
                    dve.sem_inc(prop_read, 1)
                    step(dve.tensor_tensor(v, v, dis_b, ALU.mult))
                    rows = acc[:, b * BATCH:(b + 1) * BATCH, :]
                    step(dve.tensor_tensor(rows, rows, v, ALU.add), False)
                    if layer < LAYERS - 1:
                        step(dve.tensor_tensor(v, v, dis_b, ALU.mult))
                        thirds(u1 if layer % 2 == 0 else u0, b)
            dve.wait_ge(dve_c, count[0])
            dve.sem_inc(fin_dve, 1)

            dve.wait_ge(fin_pool, 2)
            for b in range(NB):
                gs = slice(b * BATCH, (b + 1) * BATCH)
                dve.wait_ge(fin_pe, 3 * b + 2)
                step(dve.tensor_tensor(x2[:, gs, :], psf[:, 1024:1024 + BATCH * P].rearrange("p (g f) -> p g f", f=P),
                                       xb[:, gs, :], ALU.add))
                norm_stats(dve, step, x2, stats2, mv2, b * BATCH, (b + 1) * BATCH)
                dve.sem_inc(fin_dve, 1)
                dve.wait_ge(fin_act, 4 * b + 2)
                norm_scales(dve, step, mv2, small, b * BATCH, (b + 1) * BATCH)
                dve.sem_inc(fin_dve, 1)

            dve.wait_ge(ld_coef, 16)
            regs = [dve.alloc_register(f"pair{i}") for i in range(3 * U)]
            iota_w = iota16[:, 0:WIN].unsqueeze(2).broadcast_to([P, WIN, BASES])

            def operands(c, first=False):
                dve.load(regs, tab_dve[0:1, slice(c, c + 1) if isinstance(c, int) else ds(c, 1), :, :]
                         .rearrange("p c k u -> p (c k u)"))
                for u in range(U):
                    if not first and u % 5 == 0:
                        dve.wait_ge(pairs2, c * U + (u + 5 - U))
                    s = c * U + u
                    tile1 = dve.snap(regs[u], min_val=1, max_val=NT)
                    tile = dve.snap(regs[U + u], min_val=0, max_val=NT - 1)
                    slot = dve.snap(regs[2 * U + u], min_val=0, max_val=GRING - 1)
                    dve.wait_ge(gathered, tile1)
                    dve.tensor_copy(gpair[:, u:u + 1, :], gring[:, ds(slot, 1), :]).then_inc(pair_in, 1)
                    col = slice(s, s + 1) if isinstance(s, int) else ds(s, 1)
                    dve.scalar_tensor_tensor(kpair[:, u, :, :], iota_w, dlP[:, col],
                                             coef[:, ds(tile, 1), :].broadcast_to([P, WIN, BASES]),
                                             ALU.is_equal, ALU.mult).then_inc(pair_in, 1)

            operands(0, first=True)
            with dve.Fori(1, TURNS) as c:
                operands(c)

            for b in range(NB):
                gs = slice(b * BATCH, (b + 1) * BATCH)
                dve.wait_ge(tail, b + 1)
                at = (b % 2) * 1024
                dve.tensor_tensor(h2[:, gs, :], x2[:, gs, :],
                                  psf[:, at:at + BATCH * P].rearrange("p (g f) -> p g f", f=P), ALU.add).then_inc(ogrp, 1)

        @block.tensor
        def _(pe):
            pe.wait_ge(pool_c, PC0)
            pe.wait_ge(tables_in, 1)
            for h in range(2):
                for c in range(TC):
                    pe.matmul(ps[:, h, 0:HALF], ones_bf[:], stepM[:, c, h * HALF:(h + 1) * HALF],
                              start=(c == 0), stop=(c == TC - 1))
            for c in range(TC):
                last = pe.matmul(ps[:, 2, 0:NW], ones_bf[:], endM[:, c, :], start=(c == 0), stop=(c == TC - 1))
            last.then_inc(pe_setup, 1)
            pe.wait_ge(tables_in, 2)
            for k, field in enumerate((key_f, dst_f, lo_f)):
                for h in range(2):
                    for c in range(TC):
                        pe.matmul(ps[:, 2 * k + h, 0:HALF], field[:, c, :], onT[:, c, h * HALF:(h + 1) * HALF],
                                  start=(c == 0), stop=(c == TC - 1))
            for c in range(TC):
                n = min(P, NT - c * P)
                pe.matmul(ps[:, 6, c * P:c * P + n], src_f[:, c, :], ident[:, 0:n], start=True, stop=True)
            for c in range(TC):
                n = min(P, NT + 1 - c * P)
                pe.matmul(ps[:, 7, c * P:c * P + n], norm_f[:, c, :], ident[:, 0:n], start=True, stop=True)
            for c in range(TC):
                last = pe.matmul(ps[0:1, c, AT:AT + P], af[:, c:c + 1], ident[:], start=True, stop=True)
            last.then_inc(pe_setup, 1)

            pe.wait_ge(tables_in, 3)
            pe.wait_ge(ld_par, 64)
            for q in range(H_TURNS):
                n = min(4, NG - 4 * q)
                pe.wait_ge(act_c, 1 + 4 * q + n)
                if q >= 2:
                    pe.wait_ge(hcopied, q - 1)
                for i in range(n):
                    last = pe.transpose(ps[:, q % 2, i * P:(i + 1) * P], x_sb[:, 4 * q + i, :], ident[:])
                last.then_inc(htrans, 1)
                pe.wait_ge(hcopied, q + 1)
                if q >= 2:
                    pe.wait_ge(hread, q - 1)
                for i in range(n):
                    last = pe.matmul(ps[:, 2 + q % 2, i * HID:(i + 1) * HID], hT[:, q % 2, i * P:(i + 1) * P],
                                     win_sb[:], start=True, stop=True)
                last.then_inc(hmul, 1)

            pe.wait_ge(setup_over, 1)
            zb, zw = zeros[:, 0:P // 2].bitcast(BF16), zeros[:, 0:256].bitcast(BF16)
            for r in range(RING):
                pe.matmul(ps[:, r, :], zb, zw, start=True, stop=True).then_inc(slots_free, 1)

            regs = [pe.alloc_register(f"win{i}") for i in range(2 * U)]

            def slots(c):
                pe.load(regs, tab_pe[0:1, slice(c, c + 1) if isinstance(c, int) else ds(c, 1), :, :]
                        .rearrange("p c k u -> p (c k u)"))

            def count_pairs(c, b=None, first=False):
                slots(c)
                for u in range(U):
                    s = c * U + u
                    window1 = pe.snap(regs[u], min_val=1, max_val=NW + 1)
                    slot = pe.snap(regs[U + u], min_val=0, max_val=RING - 1)
                    pe.wait_ge(oh_ready, s * 2 + 2)
                    pe.wait_ge(slots_free, window1)
                    pe.matmul(ps[:, ds(slot, 1), 0:LO], ohA[:, u, :], ohB[:, u, :], start=False, stop=True,
                              skip_group_check=True).then_inc(pairs_done, 1)
                    if b is not None and u == U // 2:
                        if not first:
                            pe.wait_ge(coef_cp, c)
                        pe.wait_ge(typed, c + 1)
                        for i in range(CCH // 2):
                            both = ps[:, 4, 0:CCH * BASES].rearrange("p (h t b) -> p h t b", h=2, b=BASES)
                            last = pe.matmul(both[:, :, i, :], cbuf[:, b, i * P:(i + 1) * P], wc_sb[:],
                                             start=True, stop=True)
                        last.then_inc(coef_mm, 1)

            count_pairs(0, 0, first=True)
            with pe.Fori(0, CT_TURNS // CBUF) as q:
                for j in range(1, CBUF + 1):
                    count_pairs(q * CBUF + j, j % CBUF)
            with pe.Fori(CT_TURNS, TURNS) as c:
                count_pairs(c)

            for r in range(RING):
                pe.wait_ge(ct_in[r], 16 * NW // RING)
            for m in range(NG):
                for k in range(NG):
                    last = pe.matmul(ps[:, 7, m:m + 1], CT[:, k, m * P:(m + 1) * P], ones_bf[:, 0:1],
                                     start=(k == 0), stop=(k == NG - 1))
            last.then_inc(deg_done, 1)

            for layer in range(LAYERS):
                u = u0 if layer % 2 == 0 else u1
                pe.wait_ge(u_ready, (layer + 1) * NB)
                for b in range(NB):
                    got = layer * NB + b
                    if got >= 2:
                        pe.wait_ge(prop_read, got - 1)
                    for i in range(BATCH):
                        m = b * BATCH + i
                        at = (got % 2) * 1536 + i * SLOT
                        for k in range(NG):
                            last = pe.matmul(psf[:, at:at + PART], CT[:, k, m * P:(m + 1) * P], u[:, k, :],
                                             start=(k == 0), stop=(k == NG - 1))
                        last.then_inc(prop_done, 1)

            pe.wait_ge(fin_dve, 4)
            pe.wait_ge(ld_two, 16 * 7)
            for b in range(NB):
                for i in range(BATCH):
                    last = pe.transpose(psf[0:HID, i * P:(i + 1) * P], acc[:, b * BATCH + i, :], ident[:])
                last.then_inc(fin_pe, 1)
                pe.wait_ge(fin_act, 4 * b + 1)
                if b:
                    pe.wait_ge(fin_dve, 3 + 2 * b)
                for i in range(BATCH):
                    last = pe.matmul(psf[:, 1024 + i * P:1024 + (i + 1) * P], fT[:, i * P:(i + 1) * P], wout[:],
                                     start=True, stop=True)
                last.then_inc(fin_pe, 1)
                pe.wait_ge(fin_act, 4 * b + 3)
                for i in range(BATCH):
                    last = pe.transpose(psf[:, 2048 + i * P:2048 + (i + 1) * P], h2[:, b * BATCH + i, :], ident[:])
                last.then_inc(fin_pe, 1)

            pe.wait_ge(fin_dve, 4 + 2 * NB)
            pe.wait_ge(fin_act, 4 * NB)
            for r in range(RING):
                pe.matmul(ps[:, r, :], zb, zw, start=True, stop=True).then_inc(slots2, 1)
            greg = [pe.alloc_register(f"grp{i}") for i in range(2)]

            def group_output(g):
                half = g % 2
                pe.wait_ge(zcopied, g * WPG + WPG)
                pe.wait_ge(routed, g + 1)
                bank = ps[:, ds(half + RING, 1), 0:P].rearrange("p a n -> p (a n)")
                for b in range(BASES):
                    rows = zsb[:, ds(half, 1), :, b].rearrange("p a d -> p (a d)")
                    pe.matmul(bank, wrel[:, b, :], rows, start=(b == 0), stop=False)
                pe.matmul(bank, loopw[:], h2T[:, ds(g * P, P)], start=False, stop=True).then_inc(zgrp, 1)

            def sum_pairs(c):
                slots(c)
                for u in range(U):
                    s = c * U + u
                    window1 = pe.snap(regs[u], min_val=1, max_val=NW + 1)
                    slot = pe.snap(regs[U + u], min_val=0, max_val=RING - 1)
                    pe.wait_ge(pair_in, s * 2 + 2)
                    pe.wait_ge(slots2, window1)
                    pe.matmul(ps[:, ds(slot, 1), 0:WIN * BASES], gpair[:, u, :],
                              kpair[:, u, :, :].rearrange("p d b -> p (d b)"), start=False, stop=True,
                              skip_group_check=True).then_inc(pairs2, 1)

            with pe.Fori(0, TURNS) as c:
                sum_pairs(c)
                pe.load(greg, tab_grp[0:1, ds(c, 2)])
                done = pe.snap(greg[0], min_val=0, max_val=NG)
                now = pe.snap(greg[1], min_val=0, max_val=NG)
                with pe.If(done < now):
                    with pe.Fori(done, now) as g:
                        group_output(g)
                with pe.Else():
                    pe.nop()
            for b in range(NB):
                pe.wait_ge(routed, 2 + NG)
                if b >= 2:
                    pe.wait_ge(ogrp, b - 1)
                for i in range(BATCH):
                    at = (b % 2) * 1024 + i * P
                    last = pe.transpose(psf[:, at:at + P], relu_out[:, (b * BATCH + i) * P:(b * BATCH + i + 1) * P], ident[:])
                last.then_inc(tail, 1)

        @block.scalar
        def _(act):
            act.wait_ge(fin_dve, 1)
            act.activation(small[:, 0, :], mv[:, :, 1], ACT.Sqrt).then_inc(act_c, 1)
            act.wait_ge(fin_dve, 2)
            for g in range(NG):
                act.activation(x_sb[:, g, :], x_sb[:, g, :], ACT.Relu, bias=small[:, 1, g:g + 1],
                               scale=small[:, 0, g:g + 1]).then_inc(act_c, 1)
            for q in range(H_TURNS):
                n = min(4, NG - 4 * q)
                act.wait_ge(htrans, q + 1)
                if q >= 2:
                    act.wait_ge(hmul, q - 1)
                act.copy(hT[:, q % 2, 0:n * P], ps[:, q % 2, 0:n * P]).then_inc(hcopied, 1)

            act.wait_ge(tables_in, 3)
            wreg = [act.alloc_register(f"end{i}") for i in range(WPG)]

            def copy_windows(g, first=False):
                act.load(wreg, tab_end[0:1, slice(0, WPG) if first else ds(g * WPG, WPG)])
                for j in range(WPG):
                    act.wait_ge(pairs_done, act.snap(wreg[j], min_val=1, max_val=S))
                    if not (first and j < RING):
                        act.wait_ge(ct_in[j % RING], g * 32 + (16 if j >= RING else 0))
                    act.copy(stage[:, j % RING, :], ps[:, j % RING, 0:LO]).then_inc(staged, 1)
                    act.wait_ge(staged, g * WPG + (j + 1))
                    act.copy(ps[:, j % RING, 0:LO], zeros[:]).then_inc(slots_free, 1)

            copy_windows(0, first=True)
            with act.Fori(1, NG) as g:
                copy_windows(g)

            act.wait_ge(fin_dve, 3)
            act.activation(small[:, 4, :], small[:, 2, :], ACT.Sqrt).then_inc(act_c, 1)

            for b in range(NB):
                act.wait_ge(fin_pe, 3 * b + 1)
                act.mul(fT[:], psf[0:HID, 0:BATCH * P], 1.0 / (LAYERS + 1)).then_inc(fin_act, 1)
                act.wait_ge(fin_dve, 5 + 2 * b)
                gs = slice(b * BATCH, (b + 1) * BATCH)
                act.activation(small[:, 0, gs], mv2[:, gs, 1], ACT.Sqrt).then_inc(fin_act, 1)
                act.wait_ge(fin_dve, 6 + 2 * b)
                for i in range(BATCH):
                    g = b * BATCH + i
                    last = act.activation(h2[:, g, :], x2[:, g, :], ACT.Relu, bias=small[:, 1, g:g + 1],
                                          scale=small[:, 0, g:g + 1])
                    last.then_inc(act_n, 1)
                act.wait_ge(act_n, (b + 1) * BATCH)
                act.sem_inc(fin_act, 1)
                act.wait_ge(fin_pe, 3 * b + 3)
                act.copy(h2T[:, b * BATCH * P:(b + 1) * BATCH * P], psf[:, 2048:2048 + BATCH * P]).then_inc(fin_act, 1)

            act.sem_inc(routed, 2)

            def copy_sums(g, half, wait=True):
                act.load(wreg, tab_end[0:1, ds(g * WPG, WPG) if wait else slice(g * WPG, (g + 1) * WPG)])
                for j in range(WPG):
                    act.wait_ge(pairs2, act.snap(wreg[j], min_val=1, max_val=S))
                    act.copy(zsb[:, half, j * WIN:(j + 1) * WIN, :].rearrange("p d b -> p (d b)"),
                             ps[:, j % RING, 0:WIN * BASES]).then_inc(zcopied, 1)
                    act.wait_ge(zcopied, g * WPG + (j + 1))
                    act.copy(ps[:, j % RING, 0:WIN * BASES], zeros[:, 0:WIN * BASES]).then_inc(slots2, 1)

            def route(g, half):
                act.wait_ge(zgrp, g + 1)
                at = slice(g * P, (g + 1) * P) if isinstance(g, int) else ds(g * P, P)
                act.activation(relu_out[:, at], ps[:, RING + half, 0:P], ACT.Relu, bias=hb[:, 0:1]).then_inc(routed, 1)

            copy_sums(0, 0, False)
            copy_sums(1, 1, False)
            with act.Fori(1, NG // 2) as q:
                for half in range(2):
                    route(q * 2 + (half - 2), half)
                    copy_sums(q * 2 + half, half)
            route(NG - 3, 0)
            copy_sums(NG - 1, 0, False)
            route(NG - 2, 1)
            route(NG - 1, 0)


def norm_stats(dve, step, rows, stats, mv, lo, hi):
    for g in range(lo, hi):
        step(dve.bn_stats(stats[:, g, :], rows[:, g, :]), g == hi - 1)
    for g in range(lo, hi):
        step(dve.bn_aggr(mv[:, g, :], stats[:, g, :]), g == hi - 1)
    step(dve.tensor_scalar(mv[:, lo:hi, 1], mv[:, lo:hi, 1], EPS, None, ALU.add))


def norm_scales(dve, step, mv, small, lo, hi):
    step(dve.reciprocal(small[:, 0, lo:hi], small[:, 0, lo:hi]))
    step(dve.scalar_tensor_tensor(small[:, 1, lo:hi], mv[:, lo:hi, 0], -1.0, small[:, 0, lo:hi], ALU.mult, ALU.mult))


_ORDER = ("x", "src", "dst", "edge_type_64", "edge_weight1", "L0_gnn_W_in", "L0_gnn_b_in", "L0_gnn_W_out",
          "L0_gnn_b_out", "L1_gnn_weight", "L1_gnn_w_comp", "L1_gnn_h_bias", "L1_gnn_loop_weight")


def kernel(**inputs):
    import concourse.bacc as bacc
    from concourse.bass_utils import run_bass_kernel_spmd

    nc = bacc.Bacc("TRN2", target_bir_lowering=False, num_devices=1)
    arrays, args = {}, []
    for name in _ORDER:
        a = np.ascontiguousarray(inputs[name])
        if name == "edge_weight1":
            a = a.reshape(-1)
        arrays[name] = a
        args.append(nc.dram_tensor(name, a.shape, mybir.dt.from_np(a.dtype), kind="ExternalInput").ap())
    out = nc.dram_tensor("out", (N, FEAT), F32, kind="ExternalOutput").ap()
    build(nc, *args, out)
    return run_bass_kernel_spmd(nc, [arrays], core_ids=[0]).results[0]["out"]
```

```python
from contextlib import ExitStack

import numpy as np

import concourse.bass as bass
from concourse import mybir

F32 = mybir.dt.float32
BF16 = mybir.dt.bfloat16
I32 = mybir.dt.int32
I16 = mybir.dt.int16
U16 = mybir.dt.uint16
ALU = mybir.AluOpType
ACT = mybir.ActivationFunctionType
AX = mybir.AxisListType
ds = bass.ds

P = 128
N = 3125
E = 50000
FEAT = 128
HID = 64
BASES = 16
TYPES = 64
LAYERS = 3
EPS = 1e-5

NG = -(-N // P)
NPAD = NG * P
NT = -(-E // P)
TAIL = E - (NT - 1) * P
TC = -(-NT // P)
WIN = 16
WPG = P // WIN
NW = NG * WPG
HI = P // WIN
LO = NPAD // HI
S = NT + NW - 1
U = 10
TURNS = S // U
HALF = S // 2
RING = 4
FAR = 4095
FIELDS = 5
CCH = 8
COEF_MM, COEF_COPY = 6, 7
CHALF = CCH * P // 2
CBUF = 4
GCH = 16
CHUNKS = 4
GRING = CHUNKS * GCH
BATCH = 5
STARTS = (0, 5, 10, 15, 19, 23, NG)
NB = len(STARTS) - 1
SIZES = tuple(hi - lo for lo, hi in zip(STARTS, STARTS[1:]))
assert all(n % 2 == 0 or n == BATCH for n in SIZES)
PC0 = 11
CT_TURNS = -(-NT // CCH)
H_TURNS = -(-NG // 4)
PART = 3 * HID
AT = 320
OUT_PARTS = tuple((max(g - 4, 3), g) for g in range(NG, 3, -4)) + ((0, 3),)
SLOT = 256
DIV, DIV_SHIFT = 5243, 21
assert N * DIV < 1 << 24 and all(n * DIV >> DIV_SHIFT == n // LO for n in range(N))


def tiles_view(flat, c0, c1):
    return flat[c0 * P * P:c1 * P * P].rearrange("(c t e) -> t c e", t=P, e=P)


def build(nc, x, src, dst, etype, norm, W_in, b_in, W_out, b_out, weight, w_comp, h_bias, loop_w, out):
    assert TURNS * U == S
    ctx = ExitStack()
    with ctx:
        def sb(name, shape, dt):
            return ctx.enter_context(nc.sbuf_tensor(name, shape, dt))

        def sem(name):
            return ctx.enter_context(nc.semaphore(name))

        coef_dram = nc.dram_tensor("coef_dram", (P, CT_TURNS * CCH * BASES), F32, kind="Internal").ap()
        x2_dram = nc.dram_tensor("x2_dram", (NPAD, FEAT), F32, kind="Internal").ap()
        h2_dram = nc.dram_tensor("h2_dram", (NPAD, FEAT), F32, kind="Internal").ap()

        CT = sb("CT", [P, NG, NPAD], BF16)
        u0 = sb("u0", [P, NG, PART], BF16)
        ohbuf = sb("ohbuf", [P, U * (P + LO)], BF16)
        acc = sb("acc", [P, NG, HID], F32)
        stage = sb("stage", [P, RING, LO], BF16)
        keys = sb("keys", [P, 2 * S], F32)
        keyP, loP = keys[:, 0:S], keys[:, S:2 * S]
        dlP = sb("dlP", [P, S], F32)
        src_col = sb("src_col", [P, NT], I32)
        iota16 = sb("iota16", [P, LO], I16)
        ident = sb("ident", [P, P], F32)
        ones_bf = sb("ones_bf", [P, P], BF16)
        zeros = sb("zeros", [P, LO], F32)
        dis = sb("dis", [P, NG], F32)
        small = sb("small", [P, 5, NG], F32)
        typ = sb("typ", [P, 1], F32)
        norm_col = sb("norm_col", [P, NT + 1], F32)
        wc_sb = sb("wc_sb", [P, 2, BASES], F32)
        coef_out = sb("coef_out", [P, 2, CCH * BASES], F32)
        idx_st = sb("idx_st", [P, CHUNKS, GCH], I32)
        tab_pe = sb("tab_pe", [1, TURNS, 2 * U + 2], U16)
        tab_dve = sb("tab_dve", [1, TURNS, 3, U], U16)
        tab_end = sb("tab_end", [1, 1 + NW], U16)
        tab_tile = sb("tab_tile", [1, NT], U16)

        ohA = ohbuf[:, 0:U * P].rearrange("p (u k) -> p u k", u=U)
        ohB = ohbuf[:, U * P:].rearrange("p (u k) -> p u k", u=U)
        u1 = ohbuf[:, 0:NG * PART].rearrange("p (g k) -> p g k", g=NG)
        cbuf = u0[:, :, :].rearrange("p g k -> p (g k)")[:, 0:2 * CBUF * CHALF].bitcast(F32)
        cbuf = cbuf.rearrange("p (b e) -> p b e", b=CBUF)

        ps = ctx.enter_context(nc.psum_tensor("ps", [P, 8, 512], F32))
        psf = ps[:, :, :].rearrange("p b n -> p (b n)")

        between = ohbuf[:, 0:4 * 2 * BATCH * P].bitcast(F32).rearrange("p (k g f) -> p k g f", k=4, g=BATCH)
        x2b, h2b = between[:, 0:2], between[:, 2:4]
        at = [0]

        def carve_keys(n):
            at[0] += n
            assert at[0] <= 2 * S
            return keys[:, at[0] - n:at[0]]

        fT = carve_keys((BATCH + 1) // 2 * P)
        wout2 = carve_keys(2 * FEAT).rearrange("p (h f) -> p h f", h=2)
        bout = carve_keys(FEAT)
        stats2 = carve_keys(NG * 6).rearrange("p (g k) -> p g k", g=NG)
        mv2 = carve_keys(NG * 2).rearrange("p (g k) -> p g k", g=NG)

        late = CT[:, :, :].rearrange("p g n -> p (g n)").bitcast(F32)
        at = [0]

        def carve(n):
            at[0] += n
            assert at[0] <= late.shape[1]
            return late[:, at[0] - n:at[0]]

        dst_i = carve(TC * P).bitcast(I32).rearrange("p (c e) -> p c e", c=TC)
        src_i = carve(TC * P).bitcast(I32).rearrange("p (c e) -> p c e", c=TC)
        norm_f = carve(TC * P).rearrange("p (c e) -> p c e", c=TC)
        src_f = carve(TC * P).rearrange("p (c e) -> p c e", c=TC)
        dl_i = carve(TC * P).bitcast(I32).rearrange("p (c e) -> p c e", c=TC)
        w16_i = carve(TC * P).bitcast(I32).rearrange("p (c e) -> p c e", c=TC)
        hi_i = carve(TC * P).bitcast(I32).rearrange("p (c e) -> p c e", c=TC)
        lo_i = carve(TC * P).bitcast(I32).rearrange("p (c e) -> p c e", c=TC)
        odd_i = carve(TC * P).bitcast(I32).rearrange("p (c e) -> p c e", c=TC)
        fields = carve(FIELDS * TC * P // 2).bitcast(BF16).rearrange("p (k c e) -> p k c e", k=FIELDS, c=TC)
        iota_i = carve(S).bitcast(I32)
        iota_s = carve(S // 2).bitcast(I16)
        stepM = carve(TC * S // 2).bitcast(BF16).rearrange("p (c s) -> p c s", c=TC)
        onT = carve(TC * S // 2).bitcast(BF16).rearrange("p (c s) -> p c s", c=TC)
        ts_s = carve(S // 2).bitcast(I16)
        ws_s = carve(S // 2).bitcast(I16)
        tidx_i = carve(TC).bitcast(I32)
        tidx = carve(TC)
        wf_i = carve(TC).bitcast(I32)
        wf = carve(TC)
        af = carve(TC)
        endM = carve(TC * NW // 2).bitcast(BF16).rearrange("p (c w) -> p c w", c=TC)
        end_f = carve(1 + NW)
        rt_s = carve(S // 2).bitcast(I16)
        grpM = carve(NG * (TURNS + 1)).rearrange("p (g n) -> p g n", g=NG)
        grp_f = carve(TURNS + 1)
        turn_f = carve(TURNS + 1)
        x_sb = carve(NG * FEAT).rearrange("p (g f) -> p g f", g=NG)
        hT = carve(2 * 4 * P).rearrange("p (b n) -> p b n", b=2)
        stats = carve(NG * 6).rearrange("p (g k) -> p g k", g=NG)
        mv = carve(NG * 2).rearrange("p (g k) -> p g k", g=NG)

        typ_i = carve(1).bitcast(I32)
        win_sb = carve(HID)
        bin_sb = carve(HID)

        after = CT[:, :, :].rearrange("p g n -> p (g n)").bitcast(F32)
        at2 = [0]

        def carve2(n):
            at2[0] += n
            assert at2[0] <= after.shape[1]
            return after[:, at2[0] - n:at2[0]]

        coef = carve2(NT * BASES).rearrange("p (t b) -> p t b", b=BASES)
        wrel = carve2(BASES * FEAT).rearrange("p (b o) -> p b o", b=BASES)
        loopw = carve2(FEAT)
        hb = carve2(1)
        x2 = carve2(NG * FEAT).rearrange("p (g f) -> p g f", g=NG)
        h2 = carve2(NG * FEAT).rearrange("p (g f) -> p g f", g=NG)
        relu_out = carve2(NPAD)
        h2T = carve2(NPAD)
        gring = carve2(GRING * FEAT).rearrange("p (r f) -> p r f", r=GRING)
        gpair = carve2(U * FEAT).rearrange("p (u f) -> p u f", u=U)
        kpair = carve2(U * WIN * BASES).rearrange("p (u d b) -> p u d b", u=U, b=BASES)
        zsb = carve2(2 * P * BASES).rearrange("p (h d b) -> p h d b", h=2, b=BASES)

        v_tmp = stage[:, :, :].rearrange("p r n -> p (r n)")[:, 0:4 * BATCH * HID].bitcast(F32)
        v_tmp = v_tmp.rearrange("p (k g h) -> p k g h", k=2, g=BATCH)

        ld_dst = sem("ld_dst")
        ld_src = sem("ld_src")
        ld_norm = sem("ld_norm")
        ld_x = sem("ld_x")
        ld_par = sem("ld_par")
        pool_c = sem("pool_c")
        dve_c = sem("dve_c")
        act_c = sem("act_c")
        norm_made = sem("norm_made")
        pe_setup = sem("pe_setup")
        tables_in = sem("tables_in")
        htrans = sem("htrans")
        hcopied = sem("hcopied")
        hmul = sem("hmul")
        setup_over = sem("setup_over")
        slots_free = sem("slots_free")
        oh_ready = sem("oh_ready")
        pairs_done = sem("pairs_done")
        staged = sem("staged")
        ct_in = [sem(f"ct_in{r}") for r in range(RING)]
        et_in = [sem(f"et_in{b}") for b in range(CBUF)]
        typed = sem("typed")
        coef_mm = sem("coef_mm")
        coef_cp = sem("coef_cp")
        coef_st = [sem(f"coef_st{b}") for b in range(2)]
        passed = sem("passed")
        deg_done = sem("deg_done")
        deg_cut = sem("deg_cut")
        u_ready = sem("u_ready")
        prop_done = sem("prop_done")
        prop_read = sem("prop_read")
        tables_turned = sem("tables_turned")
        out_zero = sem("out_zero")
        ld_out = sem("ld_out")
        x_in = [sem(f"x_in{b}") for b in range(2)]
        biased = sem("biased")
        acc_done = sem("acc_done")
        acc_turned = sem("acc_turned")
        acc_c = sem("acc_c")
        acc_copied = sem("acc_copied")
        out_mm = sem("out_mm")
        x2_added = sem("x2_added")
        x2_made = sem("x2_made")
        std_made = sem("std_made")
        scales_made = sem("scales_made")
        h2_made = sem("h2_made")
        x2_st = [sem(f"x2_st{b}") for b in range(2)]
        h2_st = [sem(f"h2_st{b}") for b in range(2)]
        ld_two = sem("ld_two")
        ld_coef = sem("ld_coef")
        ld_coefs = sem("ld_coefs")
        h2_in = sem("h2_in")
        x2_in = sem("x2_in")
        h2_turned = sem("h2_turned")
        h2_copied = sem("h2_copied")
        idx_ok = sem("idx_ok")
        g_in = [sem(f"g_in{i}") for i in range(GRING)]
        gathered = sem("gathered")
        pair_in = sem("pair_in")
        slots2 = sem("slots2")
        pairs2 = sem("pairs2")
        zcopied = sem("zcopied")
        zgrp = sem("zgrp")
        routed = sem("routed")
        turned_back = sem("turned_back")
        out_ready = sem("out_ready")
        ost = sem("ost")

        block = ctx.enter_context(nc.Block())

        @block.sync
        def _(sp):
            sp.wait_ge(pool_c, 5)
            full = TC - 1
            rest = NT - 1 - full * P

            def load_rows(row, flat, signal):
                sp.dma_start(row[:, 0:full, :], tiles_view(flat, 0, full)).then_inc(signal, 16)
                sp.dma_start(row[0:rest, full, :],
                             flat[full * P * P:(NT - 1) * P].rearrange("(t e) -> t e", e=P)).then_inc(signal, 16)
                sp.dma_start(row[rest:rest + 1, full, 0:TAIL],
                             flat[(NT - 1) * P:E].rearrange("(t e) -> t e", t=1)).then_inc(signal, 16)

            load_rows(dst_i, dst, ld_dst)
            load_rows(src_i, src, ld_src)
            sp.dma_start(x_sb[:, 0:NG - 1, :], x[0:(NG - 1) * P].rearrange("(g p) f -> p g f", p=P)).then_inc(ld_x, 16)
            sp.dma_start(x_sb[0:N - (NG - 1) * P, NG - 1, :], x[(NG - 1) * P:N]).then_inc(ld_x, 16)
            load_rows(norm_f, norm, ld_norm)
            sp.dma_start(win_sb[:], W_in).then_inc(ld_par, 16)
            sp.dma_start(bin_sb[:], b_in.unsqueeze(0).broadcast_to([P, HID])).then_inc(ld_par, 16)
            for h in range(2):
                sp.dma_start(wc_sb[h * TYPES:(h + 1) * TYPES, h, :], w_comp).then_inc(ld_par, 16)

            with sp.Fori(0, NG) as g:
                for j in range(WPG):
                    sp.wait_ge(staged, g * WPG + (j + 1))
                    sp.dma_start(CT[WIN * j:WIN * (j + 1), ds(g, 1), :].rearrange("d a (h l) -> d (a h) l", h=HI),
                                 stage[:, j % RING, :]).then_inc(ct_in[j % RING], 16)

            sp.wait_ge(prop_done, (LAYERS - 1) * NG)
            sp.wait_ge(out_zero, 1)
            for h in range(2):
                sp.dma_start(wout2[h * HID:(h + 1) * HID, h, :], W_out).then_inc(ld_out, 16)
            sp.dma_start(bout, b_out.unsqueeze(0).broadcast_to([P, FEAT])).then_inc(ld_out, 16)

            def batch_rows(t, b):
                return t[STARTS[b] * P:STARTS[b + 1] * P].rearrange("(g p) f -> p g f", p=P)

            def load_x(b):
                if b < NB - 1:
                    sp.dma_start(x2b[:, b % 2, 0:SIZES[b]], batch_rows(x, b)).then_inc(x_in[b % 2], 16)
                else:
                    sp.dma_start(x2b[:, b % 2, 0:SIZES[b] - 1, :],
                                 x[STARTS[b] * P:(NG - 1) * P].rearrange("(g p) f -> p g f", p=P)).then_inc(x_in[b % 2], 16)
                    sp.dma_start(x2b[0:N - (NG - 1) * P, b % 2, SIZES[b] - 1, :], x[(NG - 1) * P:N]).then_inc(x_in[b % 2], 16)

            load_x(0)
            load_x(1)
            for b in range(NB):
                if b == NB - 2:
                    sp.wait_ge(prop_done, LAYERS * NG)
                    sp.dma_start(wrel[:], weight.rearrange("b i o -> i b o")).then_inc(ld_two, 16)
                    sp.dma_start(loopw[:], loop_w).then_inc(ld_two, 16)
                    sp.dma_start(hb[:], h_bias.unsqueeze(1)).then_inc(ld_two, 16)
                    for half in range(2):
                        sp.wait_ge(coef_st[half], 16 * ((CT_TURNS + 1 - half) // 2))
                    sp.dma_start(coef[:, NT - U:NT, :].rearrange("p t b -> p (t b)"),
                                 coef_dram[:, (NT - U) * BASES:NT * BASES]).then_inc(ld_coef, 16)
                sp.wait_ge(x2_made, b + 1)
                sp.dma_start(batch_rows(x2_dram, b), x2b[:, b % 2, 0:SIZES[b]]).then_inc(x2_st[b % 2], 16)
                sp.wait_ge(h2_made, STARTS[b + 1])
                sp.dma_start(batch_rows(h2_dram, b), h2b[:, b % 2, 0:SIZES[b]]).then_inc(h2_st[b % 2], 16)
                if b + 2 < NB:
                    sp.wait_ge(x2_st[b % 2], 16 * (b // 2 + 1))
                    load_x(b + 2)
            sp.dma_start(coef[:, 0:NT - U, :].rearrange("p t b -> p (t b)"),
                         coef_dram[:, 0:(NT - U) * BASES]).then_inc(ld_coefs, 16)
            for b in range(2):
                sp.wait_ge(h2_st[b], 16 * ((NB + 1 - b) // 2))
            sp.dma_start(h2[:], h2_dram.rearrange("(g p) f -> p g f", p=P)).then_inc(h2_in, 16)
            for b in range(2):
                sp.wait_ge(x2_st[b], 16 * ((NB + 1 - b) // 2))
            sp.dma_start(x2[:], x2_dram.rearrange("(g p) f -> p g f", p=P)).then_inc(x2_in, 16)

            with sp.Fori(0, NT // GRING) as k:
                for i in range(GRING):
                    sp.wait_ge(g_in[i], (k + 1) * 16)
                    sp.sem_inc(gathered, 1)
            for i in range(NT % GRING):
                sp.wait_ge(g_in[i], 16 * (NT // GRING + 1))
                sp.sem_inc(gathered, 1)

            for i, (lo, hi) in enumerate(OUT_PARTS):
                sp.wait_ge(out_ready, i + 1)
                whole = min(hi, N // P)
                sp.dma_start(out[lo * P:whole * P].rearrange("(g p) f -> p g f", p=P), h2[:, lo:whole, :]).then_inc(ost, 16)
                if hi > whole:
                    sp.dma_start(out[whole * P:N], h2[0:N - whole * P, whole, :]).then_inc(ost, 16)
            sp.wait_ge(ost, 16 * (len(OUT_PARTS) + 1))

        @block.gpsimd
        def _(pool):
            pool.memset(dst_i[:, TC - 1, :], FAR).then_inc(pool_c, 1)
            pool.memset(src_i[:, TC - 1, :], 0).then_inc(pool_c, 1)
            pool.memset(norm_f[:, TC - 1, :], 0.0).then_inc(pool_c, 1)
            pool.memset(x_sb[:, NG - 1, :], 0.0).then_inc(pool_c, 1)
            pool.memset(wc_sb[:], 0.0).then_inc(pool_c, 1)
            pool.iota(iota_i[:], pattern=[[1, S]], base=0, channel_multiplier=0).then_inc(pool_c, 1)
            pool.iota(tidx_i[:], pattern=[[P, TC]], base=0, channel_multiplier=1).then_inc(pool_c, 1)
            pool.memset(ident[:], 0.0).then_inc(pool_c, 1)
            pool.wait_ge(pool_c, 8)
            pool.affine_select(out=ident[:], in_=ident[:], compare_op=ALU.not_equal, fill=1.0, base=0,
                               pattern=[[-1, P]], channel_multiplier=1).then_inc(pool_c, 1)
            pool.memset(ones_bf[:], 1.0).then_inc(pool_c, 1)
            pool.memset(zeros[:], 0.0).then_inc(pool_c, 1)
            pool.wait_ge(dve_c, 2)

            def load_types(turn, b):
                lo = turn * (CCH * P)
                span = slice(lo, lo + CCH * P) if isinstance(turn, int) else ds(lo, CCH * P)
                pool.dma_start(cbuf[:, b, :].bitcast(I32),
                               etype[span].rearrange("(h e) -> h e", h=2).unsqueeze(1)
                               .broadcast_to([2, TYPES, CHALF])).then_inc(et_in[b], 16)

            def type_rows(b, loaded):
                pool.wait_ge(et_in[b], loaded)
                pool.sem_inc(passed, 1)
                pool.tensor_scalar(cbuf[:, b, :], cbuf[:, b, :].bitcast(I32), typ[:, 0:1], None,
                                   ALU.is_equal).then_inc(typed, 1)

            def store_coefs(turn, half):
                pool.wait_ge(coef_cp, turn + 1)
                at = turn * (CCH * BASES)
                span = slice(at, at + CCH * BASES) if isinstance(turn, int) else ds(at, CCH * BASES)
                pool.dma_start(coef_dram[:, span], coef_out[:, half]).then_inc(coef_st[half], 16)

            for b in range(CBUF):
                load_types(b, b)
            type_rows(0, 16)
            type_rows(1, 16)
            with pool.Fori(0, CT_TURNS // CBUF - 1) as q:
                for j in range(CBUF):
                    type_rows((j + 2) % CBUF, q * 16 + (16 * ((j + 2) // CBUF) + 16))
                    store_coefs(q * CBUF + j, j % 2)
                    load_types(q * CBUF + (j + CBUF), j)
            last = CT_TURNS - 1
            assert last % CBUF == 0
            loads = 16 * (last // CBUF)
            type_rows(2, loads)
            store_coefs(last - 4, 0)
            first_edge = last * CCH * P
            pool.dma_start(cbuf[0:TYPES, 0, :].bitcast(I32), etype[first_edge:first_edge + CHALF].unsqueeze(0)
                           .broadcast_to([TYPES, CHALF])).then_inc(et_in[0], 16)
            rest = E - first_edge - CHALF
            pool.dma_start(cbuf[TYPES:P, 0, 0:rest].bitcast(I32), etype[first_edge + CHALF:E].unsqueeze(0)
                           .broadcast_to([TYPES, rest])).then_inc(et_in[0], 16)
            type_rows(3, loads)
            store_coefs(last - 3, 1)
            type_rows(0, loads + 32)
            for turn in range(last - 2, last + 1):
                store_coefs(turn, turn % 2)

            pool.wait_ge(prop_done, 1)
            pool.memset(wout2[:], 0.0).then_inc(out_zero, 1)
            pool.wait_ge(ld_out, 48)
            for b in range(NB):
                pool.wait_ge(x_in[b % 2], 16 * (b // 2 + 1) + (16 if b == NB - 1 else 0))
                rows = x2b[:, b % 2, 0:SIZES[b]]
                pool.tensor_tensor(rows, rows, bout.unsqueeze(1).broadcast_to([P, SIZES[b], FEAT]),
                                   ALU.add).then_inc(biased, 1)

            for b in range(2):
                pool.wait_ge(h2_st[b], 16 * ((NB + 1 - b) // 2))

            def gather(k, part, n, wait):
                if wait:
                    pool.load(reg_t, tab_tile[0:1, ds(k * -GCH + (NT + GRING - GCH), 1)])
                    pool.wait_ge(pair_in, pool.snap(reg_t))
                    pool.sem_inc(passed, 1)
                src_at = ds(k * -GCH + (NT - GCH), n) if not isinstance(k, int) else slice(NT - k * GCH - n, NT - k * GCH)
                pool.tensor_copy(idx_st[:, part, 0:n], src_col[:, src_at]).then_inc(idx_ok, 1)
                pool.wait_ge(idx_ok, k + 1)
                pool.sem_inc(passed, 1)
                for i in range(n):
                    at = n - 1 - i
                    pool.indirect_dma_start(out=gring[:, part * GCH + i, :], out_offset=None, in_=h2_dram,
                                            in_offset=bass.IndirectOffsetOnAxis(ap=idx_st[:, part, at:at + 1], axis=0)
                                            ).then_inc(g_in[part * GCH + i], 16)

            reg_t = pool.alloc_register("tile_pos")
            for part in range(CHUNKS):
                gather(part, part, GCH, False)
            with pool.Fori(1, NT // GRING) as kk:
                for part in range(CHUNKS):
                    gather(kk * CHUNKS + part, part, GCH, True)
            assert NT // GRING * CHUNKS == NT // GCH
            gather(NT // GCH, 0, NT % GCH, True)

        @block.vector
        def _(dve):
            count = [0]

            def step(ins, wait=True):
                count[0] += 1
                ins.then_inc(dve_c, 1)
                if wait:
                    dve.wait_ge(dve_c, count[0])

            dve.wait_ge(pool_c, PC0)
            step(dve.tensor_single_scalar(typ_i[:], tidx_i[:, 0:1], TYPES - 1, ALU.bitwise_and))
            step(dve.tensor_copy(typ[:], typ_i[:]))
            step(dve.tensor_copy(iota_s[:], iota_i[:]), False)
            step(dve.tensor_copy(iota16[:], iota_i[:, 0:LO]), False)
            step(dve.tensor_copy(tidx[:], tidx_i[:]), False)
            dve.wait_ge(ld_dst, 16 * 3)
            step(dve.tensor_single_scalar(wf_i[:], dst_i[:, :, 0], WIN.bit_length() - 1, ALU.arith_shift_right))
            step(dve.tensor_copy(wf[:], wf_i[:]))
            step(dve.tensor_tensor(af[:], wf[:], tidx[:], ALU.add))
            step(dve.memset(af[0:1, 0:1], 0.0))
            step(dve.memset(wf[0:1, 0:1], float(FAR)))
            for c in range(TC):
                step(dve.tensor_scalar(stepM[:, c, :], iota_s[:], af[:, c:c + 1], None, ALU.is_ge), False)
                step(dve.tensor_scalar(endM[:, c, :], iota_s[:, 0:NW], wf[:, c:c + 1], None, ALU.is_ge), False)
            dve.wait_ge(dve_c, count[0])
            dve.sem_inc(tables_in, 1)
            step(dve.tensor_single_scalar(dl_i[:], dst_i[:], WIN - 1, ALU.bitwise_and), False)
            step(dve.tensor_single_scalar(w16_i[:], dst_i[:], 0xFFFF - (WIN - 1), ALU.bitwise_and), False)
            dve.wait_ge(ld_src, 16 * 3)
            step(dve.tensor_scalar(hi_i[:], src_i[:], float(DIV), None, ALU.mult))
            step(dve.tensor_single_scalar(hi_i[:], hi_i[:], DIV_SHIFT, ALU.arith_shift_right))
            step(dve.scalar_tensor_tensor(lo_i[:], hi_i[:], float(-LO), src_i[:], ALU.mult, ALU.add))
            step(dve.tensor_single_scalar(odd_i[:], lo_i[:], 1, ALU.bitwise_and))
            step(dve.tensor_copy(fields[:, 0], w16_i[:]), False)
            step(dve.tensor_copy(fields[:, 1], dl_i[:]), False)
            step(dve.tensor_copy(fields[:, 2], hi_i[:]), False)
            step(dve.tensor_tensor(fields[:, 3], lo_i[:], odd_i[:], ALU.subtract), False)
            step(dve.tensor_copy(fields[:, 4], odd_i[:]), False)
            step(dve.tensor_copy(src_f[:], src_i[:]), False)
            dve.wait_ge(pe_setup, 1)
            for h in range(2):
                step(dve.tensor_scalar(ts_s[:, h * HALF:(h + 1) * HALF], ps[:, h, 0:HALF], -1.0, None, ALU.add), False)
            step(dve.memset(end_f[:, 0:1], -1.0), False)
            step(dve.tensor_tensor(end_f[:, 1:], ps[:, 2, 0:NW], iota_s[:, 0:NW], ALU.add), False)
            dve.wait_ge(dve_c, count[0])
            for c in range(TC):
                step(dve.tensor_scalar(onT[:, c, :], ts_s[:], tidx[:, c:c + 1], None, ALU.is_equal), False)
            dve.wait_ge(dve_c, count[0])
            dve.sem_inc(tables_in, 1)
            step(dve.tensor_tensor(ws_s[:], iota_s[:], ts_s[:], ALU.subtract), False)
            dve.wait_ge(ld_x, 32)
            norm_stats(dve, step, x_sb, stats, mv, NG)
            dve.sem_inc(norm_made, 1)
            dve.wait_ge(act_c, 1)
            norm_scales(dve, step, mv, small, 0, NG)
            dve.sem_inc(norm_made, 1)
            dve.wait_ge(pe_setup, 2)
            pairs_of = lambda b: ps[:, b:b + 2, 0:HALF]
            split = lambda row: row.rearrange("p (h s) -> p h s", h=2)
            step(dve.scalar_tensor_tensor(split(dlP[:]), split(ws_s[:]), float(-WIN), pairs_of(0), ALU.mult, ALU.add))
            step(dve.scalar_tensor_tensor(split(keyP), split(dlP[:]), float(HI), pairs_of(2), ALU.mult, ALU.add), False)
            step(dve.tensor_copy(split(loP), pairs_of(4)), False)
            step(dve.tensor_copy(src_col[:], ps[:, 6, 0:NT]), False)
            step(dve.tensor_copy(norm_col[:], ps[:, 7, 0:NT + 1]), False)
            whole = (TC - 1) * P
            step(dve.tensor_scalar(tab_tile[:, 0:whole].rearrange("p (c t) -> p c t", t=P), ps[0:1, 0:TC - 1, AT:AT + P],
                                   -2.0, 2.0 * S, ALU.mult, ALU.add), False)
            step(dve.tensor_scalar(tab_tile[:, whole:NT], ps[0:1, TC - 1, AT:AT + NT - whole], -2.0, 2.0 * S,
                                   ALU.mult, ALU.add), False)
            dve.wait_ge(dve_c, count[0])
            dve.sem_inc(tables_in, 1)
            turn = lambda row: row[0:1, :].rearrange("p (c u) -> p c u", u=U)
            step(dve.tensor_scalar(tab_pe[:, :, 0:U], turn(ws_s), 1.0, None, ALU.add), False)
            step(dve.tensor_single_scalar(tab_pe[:, :, U:2 * U].bitcast(I16), turn(ws_s), RING - 1, ALU.bitwise_and), False)
            step(dve.tensor_scalar(tab_end[:], end_f[0:1, :], 1.0, None, ALU.add), False)
            step(dve.tensor_scalar(rt_s[0:1, :], ts_s[0:1, :], -1.0, float(NT - 1), ALU.mult, ALU.add))
            step(dve.tensor_scalar(tab_dve[:, :, 0, :], turn(rt_s), 1.0, None, ALU.add), False)
            step(dve.tensor_copy(tab_dve[:, :, 1, :], turn(ts_s)), False)
            step(dve.tensor_single_scalar(tab_dve[:, :, 2, :].bitcast(I16), turn(rt_s), GRING - 1, ALU.bitwise_and), False)
            step(dve.tensor_scalar(turn_f[0:1, :], iota_s[0:1, 0:TURNS + 1], float(U), -1.0, ALU.mult, ALU.add))
            starts = end_f[0:1, 0:NW].rearrange("p (g w) -> p g w", w=WPG)[:, :, 0]
            step(dve.tensor_tensor(grpM[0:1], starts.unsqueeze(2).broadcast_to([1, NG, TURNS + 1]),
                                   turn_f[0:1, :].unsqueeze(1).broadcast_to([1, NG, TURNS + 1]), ALU.is_ge))
            step(dve.tensor_reduce(grp_f[0:1, :], grpM[0:1].rearrange("p g c -> p c g"), AX.X, ALU.add))
            for i in range(2):
                step(dve.tensor_copy(tab_pe[:, :, 2 * U + i], grp_f[0:1, 1 - i:1 - i + TURNS]), False)
            dve.wait_ge(dve_c, count[0])
            dve.sem_inc(tables_in, 1)

            def finish_h():
                dve.wait_ge(ld_par, 64)
                dve.wait_ge(hmul, H_TURNS)
                for bank in range(4, 8):
                    lo = 8 * (bank - 4)
                    n = min(8, NG - lo)
                    step(dve.tensor_tensor(acc[:, lo:lo + n, :], ps[:, bank, 0:n * HID].rearrange("p (g h) -> p g h", h=HID),
                                           bin_sb[:, :].unsqueeze(1).broadcast_to([P, n, HID]), ALU.add), False)
                dve.wait_ge(dve_c, count[0])
                dve.sem_inc(setup_over, 1)

            def finish_coefs(c, half, stored):
                dve.wait_ge(coef_mm, c + 1)
                if stored is not None:
                    dve.wait_ge(coef_st[half], stored)
                tiles = slice(c * CCH, (c + 1) * CCH) if isinstance(c, int) else ds(c * CCH, CCH)
                dve.tensor_tensor(coef_out[:, half].rearrange("p (t b) -> p t b", b=BASES),
                                  ps[:, 4, 0:CCH * BASES].rearrange("p (t b) -> p t b", b=BASES),
                                  norm_col[:, tiles].unsqueeze(2).broadcast_to([P, CCH, BASES]),
                                  ALU.mult).then_inc(coef_cp, 1)

            def onehots(c, half=None, stored=None):
                first = isinstance(c, int) and c == 0
                for u in range(U):
                    if not first and u % 5 == 0:
                        dve.wait_ge(pairs_done, c * U + (u + 5 - U))
                    s = c * U + u
                    col = slice(s, s + 1) if isinstance(s, int) else ds(s, 1)
                    if u % 5 == 0:
                        cols = slice(s, s + 5) if isinstance(s, int) else ds(s, 5)
                        dve.tensor_tensor(ohA[:, u:u + 5, :], iota16[:, 0:P].unsqueeze(1).broadcast_to([P, 5, P]),
                                          keyP[:, cols].unsqueeze(2).broadcast_to([P, 5, P]),
                                          ALU.is_equal).then_inc(oh_ready, 1)
                    dve.tensor_scalar(ohB[:, u, :], iota16[:], loP[:, col], None, ALU.is_equal).then_inc(oh_ready, 1)
                    if half is not None and u == COEF_COPY:
                        finish_coefs(c - 1, half, stored)

            onehots(0)
            finish_h()
            onehots(1, 0)
            onehots(2, 1)
            with dve.Fori(0, CT_TURNS // 2 - 1) as q:
                for half in range(2):
                    onehots(q * 2 + (half + 3), half, q * 16 + 16)
            assert CT_TURNS % 2 == 1
            onehots(CT_TURNS, 0, 16 * (CT_TURNS // 2))
            with dve.Fori(CT_TURNS + 1, TURNS) as c:
                onehots(c)

            dve.wait_ge(deg_done, 1)
            deg = ps[:, 7, 0:NG]
            step(dve.tensor_scalar(small[:, 2, :], deg, 1.0, None, ALU.max))
            dve.sem_inc(deg_cut, 1)
            step(dve.tensor_scalar(small[:, 3, :], deg, 0.0, None, ALU.is_gt), False)
            dve.wait_ge(act_c, 2 + NG)
            step(dve.reciprocal(small[:, 4, :], small[:, 4, :]))
            step(dve.tensor_tensor(dis[:], small[:, 4, :], small[:, 3, :], ALU.mult))

            def scaled(k, b):
                return v_tmp[:, k, 0:SIZES[b]], dis[:, STARTS[b]:STARTS[b + 1]].unsqueeze(2).broadcast_to([P, SIZES[b], HID])

            def thirds(u, b):
                rows = u[:, STARTS[b]:STARTS[b + 1], :].rearrange("p g (k h) -> p g k h", k=3)
                v, r = v_tmp[:, 0, 0:SIZES[b]], v_tmp[:, 1, 0:SIZES[b]]
                step(dve.tensor_copy(rows[:, :, 0, :], v))
                step(dve.tensor_tensor(r, v, rows[:, :, 0, :], ALU.subtract))
                step(dve.tensor_copy(rows[:, :, 1, :], r))
                step(dve.tensor_tensor(rows[:, :, 2, :], r, rows[:, :, 1, :], ALU.subtract))
                dve.sem_inc(u_ready, 1)

            for b in range(NB):
                v, dis_b = scaled(0, b)
                step(dve.tensor_tensor(v, acc[:, STARTS[b]:STARTS[b + 1], :], dis_b, ALU.mult))
                thirds(u0, b)
            step(dve.tensor_scalar(tab_pe[:, :, 0:U], tab_pe[:, :, 0:U], -1.0, NW + 1.0, ALU.mult, ALU.add), False)
            step(dve.tensor_scalar(tab_end[:], tab_end[:], -1.0, float(S), ALU.mult, ALU.add), False)
            dve.wait_ge(dve_c, count[0])
            dve.sem_inc(tables_turned, 1)

            def between_blocks(b):
                dve.wait_ge(out_mm, b + 1)
                dve.wait_ge(biased, b + 1)
                rows = x2b[:, b % 2, 0:SIZES[b]]
                even = SIZES[b] // 2 * 2
                step(dve.tensor_tensor(rows[:, 0:even, :], ps[:, 7, 0:even * P].rearrange("p (g f) -> p g f", f=FEAT),
                                       rows[:, 0:even, :], ALU.add), False)
                if even < SIZES[b]:
                    step(dve.tensor_tensor(rows[:, even, :], ps[:, 6, 3 * P:4 * P], rows[:, even, :], ALU.add), False)
                dve.wait_ge(dve_c, count[0])
                dve.sem_inc(x2_added, 1)
                gs = slice(STARTS[b], STARTS[b + 1])
                norm_stats(dve, step, rows, stats2[:, gs, :], mv2[:, gs, :], SIZES[b])
                dve.sem_inc(x2_made, 1)
                dve.wait_ge(std_made, b + 1)
                norm_scales(dve, step, mv2, small, STARTS[b], STARTS[b + 1])
                dve.sem_inc(scales_made, 1)

            for layer in range(LAYERS):
                for b in range(NB):
                    got = layer * NB + b
                    dve.wait_ge(prop_done, layer * NG + STARTS[b + 1])
                    sums = psf[:, (got % 2) * 1536:(got % 2) * 1536 + SIZES[b] * SLOT].rearrange(
                        "p (g k) -> p g k", k=SLOT)
                    v, dis_b = scaled(0, b)
                    r = v_tmp[:, 1, 0:SIZES[b]]
                    step(dve.tensor_copy(r, sums[:, :, 2 * HID:3 * HID]))
                    step(dve.tensor_tensor(r, sums[:, :, HID:2 * HID], r, ALU.add))
                    step(dve.tensor_tensor(v, sums[:, :, 0:HID], r, ALU.add))
                    dve.sem_inc(prop_read, 1)
                    step(dve.tensor_tensor(v, v, dis_b, ALU.mult))
                    rows = acc[:, STARTS[b]:STARTS[b + 1], :]
                    step(dve.tensor_tensor(rows, rows, v, ALU.add), False)
                    if layer < LAYERS - 1:
                        step(dve.tensor_tensor(v, v, dis_b, ALU.mult))
                        thirds(u1 if layer % 2 == 0 else u0, b)
                    else:
                        dve.wait_ge(dve_c, count[0])
                        dve.sem_inc(acc_done, 1)
                        if b:
                            between_blocks(b - 1)
            between_blocks(NB - 1)

            dve.wait_ge(ld_coef, 16)
            regs = [dve.alloc_register(f"pair{i}") for i in range(3 * U)]
            iota_w = iota16[:, 0:WIN].unsqueeze(2).broadcast_to([P, WIN, BASES])

            def operands(c, first=False):
                row = slice(TURNS - 1 - c, TURNS - c) if isinstance(c, int) else ds(c * -1 + (TURNS - 1), 1)
                dve.load(regs, tab_dve[0:1, row, :, :].rearrange("p c k u -> p (c k u)"))
                for u in range(U):
                    if not first and u % 2 == 0:
                        dve.wait_ge(pairs2, c * U + (u + 2 - U))
                    back = U - 1 - u
                    s = c * -U + (S - 1 - u)
                    tiles = dve.snap(regs[back], min_val=1, max_val=NT)
                    tile = dve.snap(regs[U + back], min_val=0, max_val=NT - 1)
                    slot = dve.snap(regs[2 * U + back], min_val=0, max_val=GRING - 1)
                    dve.wait_ge(gathered, tiles)
                    dve.tensor_copy(gpair[:, u:u + 1, :], gring[:, ds(slot, 1), :]).then_inc(pair_in, 1)
                    col = slice(s, s + 1) if isinstance(s, int) else ds(s, 1)
                    dve.scalar_tensor_tensor(kpair[:, u, :, :], iota_w, dlP[:, col],
                                             coef[:, ds(tile, 1), :].broadcast_to([P, WIN, BASES]),
                                             ALU.is_equal, ALU.mult).then_inc(pair_in, 1)

            operands(0, first=True)
            dve.wait_ge(ld_coefs, 16)
            with dve.Fori(1, TURNS - 1) as c:
                operands(c)

            def add_x2(i):
                lo, hi = OUT_PARTS[i]
                dve.wait_ge(turned_back, i + 1)
                dve.tensor_tensor(h2[:, lo:hi, :], x2[:, lo:hi, :],
                                  ps[:, 6 + i % 2, 0:(hi - lo) * P].rearrange("p (g f) -> p g f", f=P),
                                  ALU.add).then_inc(out_ready, 1)

            dve.wait_ge(x2_in, 16)
            for i in range(len(OUT_PARTS) - 1):
                add_x2(i)
            operands(TURNS - 1)
            add_x2(len(OUT_PARTS) - 1)

        @block.tensor
        def _(pe):
            pe.wait_ge(pool_c, PC0)
            pe.wait_ge(tables_in, 1)
            for h in range(2):
                for c in range(TC):
                    pe.matmul(ps[:, h, 0:HALF], ones_bf[:], stepM[:, c, h * HALF:(h + 1) * HALF],
                              start=(c == 0), stop=(c == TC - 1))
            for c in range(TC):
                last = pe.matmul(ps[:, 2, 0:NW], ones_bf[:], endM[:, c, :], start=(c == 0), stop=(c == TC - 1))
            last.then_inc(pe_setup, 1)
            pe.wait_ge(tables_in, 2)
            for bank, parts in ((0, (0, 1)), (2, (2,)), (4, (3, 4))):
                for h in range(2):
                    for k in parts:
                        for c in range(TC):
                            pe.matmul(ps[:, bank + h, 0:HALF], fields[:, k, c, :], onT[:, c, h * HALF:(h + 1) * HALF],
                                      start=(k == parts[0] and c == 0), stop=(k == parts[-1] and c == TC - 1))
            for c in range(TC):
                n = min(P, NT - c * P)
                pe.matmul(ps[:, 6, c * P:c * P + n], src_f[:, c, :], ident[:, 0:n], start=True, stop=True)
            pe.wait_ge(ld_norm, 16 * 3)
            for c in range(TC):
                n = min(P, NT + 1 - c * P)
                pe.matmul(ps[:, 7, c * P:c * P + n], norm_f[:, c, :], ident[:, 0:n], start=True, stop=True)
            for c in range(TC):
                last = pe.matmul(ps[0:1, c, AT:AT + P], af[:, c:c + 1], ident[:], start=True, stop=True)
            last.then_inc(pe_setup, 1)

            pe.wait_ge(tables_in, 3)
            pe.wait_ge(ld_par, 64)
            def turn_x(q):
                n = min(4, NG - 4 * q)
                pe.wait_ge(act_c, 1 + 4 * q + n)
                if q >= 2:
                    pe.wait_ge(hcopied, q - 1)
                for i in range(n):
                    last = pe.transpose(ps[:, q % 2, i * P:(i + 1) * P], x_sb[:, 4 * q + i, :], ident[:])
                last.then_inc(htrans, 1)

            turn_x(0)
            for q in range(H_TURNS):
                if q + 1 < H_TURNS:
                    turn_x(q + 1)
                pe.wait_ge(hcopied, q + 1)
                n = min(4, NG - 4 * q)
                for i in range(n):
                    at = (q % 2 * 4 + i) * HID
                    last = pe.matmul(ps[:, 4 + q // 2, at:at + HID], hT[:, q % 2, i * P:(i + 1) * P],
                                     win_sb[:], start=True, stop=True)
                last.then_inc(hmul, 1)
            pe.wait_ge(tables_in, 4)

            pe.wait_ge(setup_over, 1)
            zb, zw = zeros[:, 0:P // 2].bitcast(BF16), zeros[:, 0:256].bitcast(BF16)
            for r in range(RING):
                pe.matmul(ps[:, r, :], zb, zw, start=True, stop=True).then_inc(slots_free, 1)

            regs = [pe.alloc_register(f"win{i}") for i in range(2 * U)]

            def slots(c, regs):
                pe.load(regs, tab_pe[0:1, slice(c, c + 1) if isinstance(c, int) else ds(c, 1), 0:len(regs)]
                        .rearrange("p c k -> p (c k)"))

            def count_pairs(c, b=None, first=False):
                slots(c, regs)
                for u in range(U):
                    s = c * U + u
                    slot = pe.snap(regs[U + u], min_val=0, max_val=RING - 1)
                    if u % 2 == 0:
                        window1 = pe.snap(regs[u + 1], min_val=1, max_val=NW + 1)
                        pe.wait_ge(oh_ready, c * (U + 2) + ((u + 2) + ((u + 1) // 5 + 1)))
                        pe.wait_ge(slots_free, window1)
                    pe.matmul(ps[:, ds(slot, 1), 0:LO], ohA[:, u, :], ohB[:, u, :], start=False, stop=True,
                              skip_group_check=True).then_inc(pairs_done, 1)
                    if b is not None and u == COEF_MM:
                        if not first:
                            pe.wait_ge(coef_cp, c)
                        pe.wait_ge(typed, c + 1)
                        for i in range(CCH // 2):
                            both = ps[:, 4, 0:CCH * BASES].rearrange("p (h t b) -> p h t b", h=2, b=BASES)
                            last = pe.matmul(both[:, :, i, :], cbuf[:, b, i * P:(i + 1) * P], wc_sb[:],
                                             start=True, stop=True)
                        last.then_inc(coef_mm, 1)

            count_pairs(0, 0, first=True)
            with pe.Fori(0, CT_TURNS // CBUF) as q:
                for j in range(1, CBUF + 1):
                    count_pairs(q * CBUF + j, j % CBUF)

            def add_degrees(k):
                for r in range(RING):
                    pe.wait_ge(ct_in[r], 16 * (k + 1) * (WPG // RING))
                for m in range(NG):
                    last = pe.matmul(ps[:, 7, m:m + 1], CT[:, k, m * P:(m + 1) * P], ones_bf[:, 0:1],
                                     start=False, stop=True, skip_group_check=True)
                return last

            pe.matmul(ps[:, 7, :], zb, zw, start=True, stop=True)
            for c in range(CT_TURNS, TURNS):
                count_pairs(c)
                assert (c - CT_TURNS + 1) * 2 * WPG <= c * U - NT
                for k in range((c - CT_TURNS) * 2, (c - CT_TURNS + 1) * 2):
                    add_degrees(k)
            for k in range((TURNS - CT_TURNS) * 2, NG):
                last = add_degrees(k)
            last.then_inc(deg_done, 1)

            def turn_acc(b):
                pe.wait_ge(acc_done, b + 1)
                if b:
                    pe.wait_ge(x2_added, b)
                for i in range(0, SIZES[b], 2):
                    n = min(2, SIZES[b] - i)
                    rows = acc[:, STARTS[b] + i:STARTS[b] + i + n, :].rearrange("p g h -> p (g h)")
                    last = pe.transpose(ps[0:n * HID, 6, i // 2 * P:(i // 2 + 1) * P], rows, ident[:])
                last.then_inc(acc_turned, 1)

            def times_w_out(b):
                pe.wait_ge(acc_copied, b + 1)
                for k in range(SIZES[b] // 2):
                    last = pe.matmul(ps[:, 7, k * 2 * P:(k + 1) * 2 * P], fT[:, k * P:(k + 1) * P],
                                     wout2[:].rearrange("p h f -> p (h f)"), start=True, stop=True)
                if SIZES[b] % 2:
                    last = pe.matmul(ps[:, 6, 3 * P:4 * P], fT[0:HID, 2 * P:3 * P], wout2[0:HID, 0, :],
                                     start=True, stop=True)
                last.then_inc(out_mm, 1)

            for layer in range(LAYERS):
                u = u0 if layer % 2 == 0 else u1
                for b in range(NB):
                    got = layer * NB + b
                    if got >= 2:
                        pe.wait_ge(prop_read, got - 1)

                    def sums(i, lo, hi):
                        m = STARTS[b] + i
                        at = (got % 2) * 1536 + i * SLOT
                        for k in range(lo, hi):
                            ins = pe.matmul(psf[:, at:at + PART], CT[:, k, m * P:(m + 1) * P], u[:, k, :],
                                            start=(k == 0), stop=(k == NG - 1))
                        if hi == NG:
                            ins.then_inc(prop_done, 1)

                    if b == 0:
                        for part in range(NB):
                            pe.wait_ge(u_ready, layer * NB + part + 1)
                            for i in range(0, SIZES[b], 2):
                                sums(i, STARTS[part], STARTS[part + 1])
                        for i in range(1, SIZES[b], 2):
                            sums(i, 0, NG)
                    else:
                        for i in range(SIZES[b]):
                            sums(i, 0, NG)
                            if layer == LAYERS - 1 and i == min(2, SIZES[b] - 1):
                                if b == 1:
                                    pe.wait_ge(ld_out, 48)
                                turn_acc(b - 1)
                            if layer == LAYERS - 1 and i == SIZES[b] - 1:
                                times_w_out(b - 1)
            turn_acc(NB - 1)
            times_w_out(NB - 1)

            pe.wait_ge(x2_made, NB)
            for r in range(RING):
                pe.matmul(ps[:, r, :], zb, zw, start=True, stop=True).then_inc(slots2, 1)
            pe.wait_ge(h2_in, 16)
            for b in range(NG // BATCH):
                if b >= 2:
                    pe.wait_ge(h2_copied, b - 1)
                for i in range(BATCH):
                    at = 2048 + (b % 2) * 1024 + i * P
                    last = pe.transpose(psf[:, at:at + P], h2[:, b * BATCH + i, :], ident[:])
                last.then_inc(h2_turned, 1)
            pe.wait_ge(h2_copied, NG // BATCH)
            pe.wait_ge(ld_two, 48)
            pe.wait_ge(tables_turned, 1)
            greg = [pe.alloc_register(f"grp{i}") for i in range(2)]

            def group_output(g):
                half = g % 2
                pe.wait_ge(zcopied, g * WPG + WPG)
                pe.wait_ge(routed, g + 1)
                bank = ps[:, ds(half + RING, 1), 0:P].rearrange("p a n -> p (a n)")
                for b in range(BASES):
                    rows = zsb[:, ds(half, 1), :, b].rearrange("p a d -> p (a d)")
                    pe.matmul(bank, wrel[:, b, :], rows, start=(b == 0), stop=False)
                pe.matmul(bank, loopw[:], h2T[:, ds(g * -P + (NG - 1) * P, P)], start=False, stop=True).then_inc(zgrp, 1)

            def sum_pairs(c):
                slots(TURNS - 1 - c if isinstance(c, int) else c * -1 + (TURNS - 1), regs + greg)
                for u in range(U):
                    back = U - 1 - u
                    slot = pe.snap(regs[U + back], min_val=0, max_val=RING - 1)
                    if u % 2 == 0:
                        windows = pe.snap(regs[back - 1], min_val=1, max_val=NW)
                        pe.wait_ge(pair_in, (c * U + u) * 2 + 4)
                        pe.wait_ge(slots2, windows)
                    pe.matmul(ps[:, ds(slot, 1), 0:WIN * BASES], gpair[:, u, :],
                              kpair[:, u, :, :].rearrange("p d b -> p (d b)"), start=False, stop=True,
                              skip_group_check=True).then_inc(pairs2, 1)

            def complete_groups():
                done = pe.snap(greg[0], min_val=0, max_val=NG)
                now = pe.snap(greg[1], min_val=0, max_val=NG)
                with pe.If(done < now):
                    with pe.Fori(done, now) as g:
                        group_output(g)
                with pe.Else():
                    pe.nop()

            def turn_back(i):
                lo, hi = OUT_PARTS[i]
                pe.wait_ge(routed, 2 + NG - lo)
                if i >= 2:
                    pe.wait_ge(out_ready, i - 1)
                for g in range(lo, hi):
                    last = pe.transpose(ps[:, 6 + i % 2, (g - lo) * P:(g - lo + 1) * P],
                                        relu_out[:, g * P:(g + 1) * P], ident[:])
                last.then_inc(turned_back, 1)

            with pe.Fori(0, TURNS - 1) as c:
                sum_pairs(c)
                complete_groups()
            assert OUT_PARTS[-2][0] * WPG >= U
            for i in range(len(OUT_PARTS) - 1):
                turn_back(i)
            sum_pairs(TURNS - 1)
            with pe.Fori(pe.snap(greg[0], min_val=0, max_val=NG - 1), NG) as g:
                group_output(g)
            turn_back(len(OUT_PARTS) - 1)

        @block.scalar
        def _(act):
            act.wait_ge(norm_made, 1)
            act.activation(small[:, 0, :], mv[:, :, 1], ACT.Sqrt).then_inc(act_c, 1)
            act.wait_ge(norm_made, 2)
            def copy_turned(q):
                n = min(4, NG - 4 * q)
                act.wait_ge(htrans, q + 1)
                if q >= 2:
                    act.wait_ge(hmul, q - 1)
                act.copy(hT[:, q % 2, 0:n * P], ps[:, q % 2, 0:n * P]).then_inc(hcopied, 1)

            for g in range(NG):
                act.activation(x_sb[:, g, :], x_sb[:, g, :], ACT.Relu, bias=small[:, 1, g:g + 1],
                               scale=small[:, 0, g:g + 1]).then_inc(act_c, 1)
                if g % 4 == 3 and g > 4:
                    copy_turned(g // 4 - 1)
            for q in range(NG // 4 - 1, H_TURNS):
                copy_turned(q)

            act.wait_ge(tables_in, 4)
            wreg = [act.alloc_register(f"end{i}") for i in range(WPG)]

            def copy_windows(g, first=False):
                act.load(wreg, tab_end[0:1, slice(1, WPG + 1) if first else ds(g * WPG + 1, WPG)])
                for j in range(WPG):
                    act.wait_ge(pairs_done, act.snap(wreg[j], min_val=1, max_val=S))
                    if not (first and j < RING):
                        act.wait_ge(ct_in[j % RING], g * 32 + (16 if j >= RING else 0))
                    act.copy(stage[:, j % RING, :], ps[:, j % RING, 0:LO]).then_inc(staged, 1)
                    act.wait_ge(staged, g * WPG + (j + 1))
                    act.copy(ps[:, j % RING, 0:LO], zeros[:]).then_inc(slots_free, 1)

            copy_windows(0, first=True)
            with act.Fori(1, NG) as g:
                copy_windows(g)

            act.wait_ge(deg_cut, 1)
            act.activation(small[:, 4, :], small[:, 2, :], ACT.Sqrt).then_inc(act_c, 1)

            def copy_acc(b):
                act.wait_ge(acc_turned, b + 1)
                if b:
                    act.wait_ge(out_mm, b)
                n = SIZES[b] // 2 * P
                act.mul(fT[:, 0:n], ps[:, 6, 0:n], 1.0 / (LAYERS + 1)).then_inc(acc_c, 1)
                if SIZES[b] % 2:
                    act.mul(fT[0:HID, n:n + P], ps[0:HID, 6, n:n + P], 1.0 / (LAYERS + 1)).then_inc(acc_c, 1)
                act.wait_ge(acc_c, sum(1 + n % 2 for n in SIZES[0:b + 1]))
                act.sem_inc(acc_copied, 1)

            def make_h2(b):
                act.wait_ge(x2_made, b + 1)
                gs = slice(STARTS[b], STARTS[b + 1])
                act.activation(small[:, 0, gs], mv2[:, gs, 1], ACT.Sqrt).then_inc(std_made, 1)
                act.wait_ge(scales_made, b + 1)
                if b >= 2:
                    act.wait_ge(h2_st[b % 2], 16 * (b // 2))
                for i in range(SIZES[b]):
                    g = STARTS[b] + i
                    act.activation(h2b[:, b % 2, i, :], x2b[:, b % 2, i, :], ACT.Relu, bias=small[:, 1, g:g + 1],
                                   scale=small[:, 0, g:g + 1]).then_inc(h2_made, 1)

            for b in range(NB):
                copy_acc(b)
                if b:
                    make_h2(b - 1)
            make_h2(NB - 1)
            for b in range(NG // BATCH):
                act.wait_ge(h2_turned, b + 1)
                at = 2048 + (b % 2) * 1024
                act.copy(h2T[:, b * BATCH * P:(b + 1) * BATCH * P], psf[:, at:at + BATCH * P]).then_inc(h2_copied, 1)

            act.sem_inc(routed, 2)

            def copy_sums(k, half):
                first = (NG - 1 - k) * WPG if isinstance(k, int) else k * -WPG + (NG - 1) * WPG
                act.load(wreg, tab_end[0:1, slice(first, first + WPG) if isinstance(k, int) else ds(first, WPG)])
                for i in range(WPG):
                    j = WPG - 1 - i
                    act.wait_ge(pairs2, act.snap(wreg[j], min_val=1, max_val=S))
                    act.copy(zsb[:, half, j * WIN:(j + 1) * WIN, :].rearrange("p d b -> p (d b)"),
                             ps[:, j % RING, 0:WIN * BASES]).then_inc(zcopied, 1)
                    act.wait_ge(zcopied, k * WPG + (i + 1))
                    act.copy(ps[:, j % RING, 0:WIN * BASES], zeros[:, 0:WIN * BASES]).then_inc(slots2, 1)

            def route(k, half):
                act.wait_ge(zgrp, k + 1)
                at = slice((NG - 1 - k) * P, (NG - k) * P) if isinstance(k, int) else ds(k * -P + (NG - 1) * P, P)
                act.activation(relu_out[:, at], ps[:, RING + half, 0:P], ACT.Relu, bias=hb[:, 0:1]).then_inc(routed, 1)

            act.wait_ge(tables_turned, 1)
            copy_sums(0, 0)
            copy_sums(1, 1)
            with act.Fori(1, NG // 2) as q:
                for half in range(2):
                    route(q * 2 + (half - 2), half)
                    copy_sums(q * 2 + half, half)
            route(NG - 3, 0)
            copy_sums(NG - 1, 0)
            route(NG - 2, 1)
            route(NG - 1, 0)


def norm_stats(dve, step, rows, stats, mv, n):
    for g in range(n):
        step(dve.bn_stats(stats[:, g, :], rows[:, g, :]), g == n - 1)
    for g in range(n):
        step(dve.bn_aggr(mv[:, g, :], stats[:, g, :]), g == n - 1)
    step(dve.tensor_scalar(mv[:, 0:n, 1], mv[:, 0:n, 1], EPS, None, ALU.add))


def norm_scales(dve, step, mv, small, lo, hi):
    step(dve.reciprocal(small[:, 0, lo:hi], small[:, 0, lo:hi]))
    step(dve.scalar_tensor_tensor(small[:, 1, lo:hi], mv[:, lo:hi, 0], -1.0, small[:, 0, lo:hi], ALU.mult, ALU.mult))


_ORDER = ("x", "src", "dst", "edge_type_64", "edge_weight1", "L0_gnn_W_in", "L0_gnn_b_in", "L0_gnn_W_out",
          "L0_gnn_b_out", "L1_gnn_weight", "L1_gnn_w_comp", "L1_gnn_h_bias", "L1_gnn_loop_weight")


def kernel(**inputs):
    import concourse.bacc as bacc
    from concourse.bass_utils import run_bass_kernel_spmd

    nc = bacc.Bacc("TRN2", target_bir_lowering=False, num_devices=1)
    arrays, args = {}, []
    for name in _ORDER:
        a = np.ascontiguousarray(inputs[name])
        if name == "edge_weight1":
            a = a.reshape(-1)
        arrays[name] = a
        args.append(nc.dram_tensor(name, a.shape, mybir.dt.from_np(a.dtype), kind="ExternalInput").ap())
    out = nc.dram_tensor("out", (N, FEAT), F32, kind="ExternalOutput").ap()
    build(nc, *args, out)
    return run_bass_kernel_spmd(nc, [arrays], core_ids=[0]).results[0]["out"]
```
